# Optimizing a Trainium2 kernel written in Bass

```python
import numpy as np
import jax
import jax.numpy as jnp

def _softmax(x, axis=-1):
    return jax.nn.softmax(x, axis=axis)

def _gelu(x):
    return jax.nn.gelu(x, approximate=True)

def _silu(x):
    return jax.nn.silu(x)

def _sigmoid(x):
    return jax.nn.sigmoid(x)

def _layernorm(x, axis=-1, eps=1e-05):
    m = jnp.mean(x, axis=axis, keepdims=True)
    v = jnp.var(x, axis=axis, keepdims=True)
    return (x - m) / jnp.sqrt(v + eps)

def _scatter_add(tgt, idx, src, axis=0):
    return tgt.at[idx].add(src)

def _segment_sum(src, seg, n):
    return jax.ops.segment_sum(src, seg, n)
kernel_name = 'mk_seq_preln_d1_jaxref_r8_db6601'

def setup_inputs(seed: int=0):
    np.random.seed(seed)
    _w = jnp.asarray

    def _L0_attn_setup():
        import math
        import jax, jax.numpy as jnp
        import numpy as np
        D_MODEL = 512
        N_HEADS = 32
        N_KV_HEADS = 8
        D_HEAD = D_MODEL // N_HEADS
        GROUP = N_HEADS // N_KV_HEADS
        ROPE = dict(rope_theta=500000.0, factor=32.0, hi_freq_factor=4.0, lo_freq_factor=1.0, original_context_length=1024)

        def _rope_cos_sin(head_dim, pos, dtype):
            idx = jnp.arange(0, head_dim, 2, dtype=jnp.float32) / head_dim
            freq = 1.0 / (2.0 * math.pi) * ROPE['rope_theta'] ** (-idx)
            factor, lo, hi = (ROPE['factor'], ROPE['lo_freq_factor'], ROPE['hi_freq_factor'])
            L0 = ROPE['original_context_length']
            freq_low, freq_high = (lo / L0, hi / L0)
            freq_scaled = jnp.where(freq < freq_low, freq / factor, freq)
            smooth = jnp.clip((L0 * freq - lo) / (hi - lo), 0.0, 1.0)
            freq_smooth = (1.0 - smooth) * (freq / factor) + smooth * freq
            is_mid = (freq >= freq_low) & (freq <= freq_high)
            freq = jnp.where(is_mid, freq_smooth, freq_scaled)
            phase = 2.0 * math.pi * pos.astype(jnp.float32)[:, None] * freq[None, :]
            emb = jnp.concatenate([phase, phase], axis=-1)
            return (jnp.cos(emb).astype(dtype), jnp.sin(emb).astype(dtype))

        def _rotate_half(x):
            h = x.shape[-1] // 2
            return jnp.concatenate([-x[..., h:], x[..., :h]], axis=-1)
        key = jax.random.key(seed)
        ks = jax.random.split(key, 5)
        B, T = (1, 256)
        s = 0.02
        return {'resid': jax.random.normal(ks[0], (B, T, D_MODEL), jnp.float32), 'Wq': jax.random.normal(ks[1], (D_MODEL, D_MODEL), jnp.float32) * s, 'Wk': jax.random.normal(ks[2], (D_MODEL, N_KV_HEADS * D_HEAD), jnp.float32) * s, 'Wv': jax.random.normal(ks[3], (D_MODEL, N_KV_HEADS * D_HEAD), jnp.float32) * s, 'Wo': jax.random.normal(ks[4], (D_MODEL, D_MODEL), jnp.float32) * s}
    _L0_attn_in = _L0_attn_setup()

    def _L0_ffn_setup():
        import jax, jax.numpy as jnp
        import numpy as np
        D = 512
        F = 1376
        B, S = (4, 256)
        key = jax.random.key(seed)
        k_x, k_g, k_u, k_d = jax.random.split(key, 4)
        scale = 0.02
        return {'x': jax.random.normal(k_x, (B, S, D), dtype=jnp.float32), 'W_gate': jax.random.normal(k_g, (F, D), dtype=jnp.float32) * scale, 'W_up': jax.random.normal(k_u, (F, D), dtype=jnp.float32) * scale, 'W_down': jax.random.normal(k_d, (D, F), dtype=jnp.float32) * scale}
    _L0_ffn_in = _L0_ffn_setup()
    _d = {'L0_attn_resid': _L0_attn_in['resid'], 'L0_attn_Wq': _L0_attn_in['Wq'], 'L0_attn_Wk': _L0_attn_in['Wk'], 'L0_attn_Wv': _L0_attn_in['Wv'], 'L0_attn_Wo': _L0_attn_in['Wo'], 'L0_ffn_W_gate': _L0_ffn_in['W_gate'], 'L0_ffn_W_up': _L0_ffn_in['W_up'], 'L0_ffn_W_down': _L0_ffn_in['W_down']}
    _x0 = _d['L0_attn_resid']
    _d['L0_attn_resid'] = jax.random.normal(jax.random.fold_in(jax.random.key(seed), 1), (4, 512, 512), dtype=_x0.dtype)
    del _x0
    return _d

def reference(L0_attn_resid, L0_attn_Wq, L0_attn_Wk, L0_attn_Wv, L0_attn_Wo, L0_ffn_W_gate, L0_ffn_W_up, L0_ffn_W_down):

    def _L0_attn_ref(resid, Wq, Wk, Wv, Wo):
        import math
        import jax, jax.numpy as jnp
        import numpy as np
        D_MODEL = 512
        N_HEADS = 32
        N_KV_HEADS = 8
        D_HEAD = D_MODEL // N_HEADS
        GROUP = N_HEADS // N_KV_HEADS
        ROPE = dict(rope_theta=500000.0, factor=32.0, hi_freq_factor=4.0, lo_freq_factor=1.0, original_context_length=1024)

        def _rope_cos_sin(head_dim, pos, dtype):
            idx = jnp.arange(0, head_dim, 2, dtype=jnp.float32) / head_dim
            freq = 1.0 / (2.0 * math.pi) * ROPE['rope_theta'] ** (-idx)
            factor, lo, hi = (ROPE['factor'], ROPE['lo_freq_factor'], ROPE['hi_freq_factor'])
            L0 = ROPE['original_context_length']
            freq_low, freq_high = (lo / L0, hi / L0)
            freq_scaled = jnp.where(freq < freq_low, freq / factor, freq)
            smooth = jnp.clip((L0 * freq - lo) / (hi - lo), 0.0, 1.0)
            freq_smooth = (1.0 - smooth) * (freq / factor) + smooth * freq
            is_mid = (freq >= freq_low) & (freq <= freq_high)
            freq = jnp.where(is_mid, freq_smooth, freq_scaled)
            phase = 2.0 * math.pi * pos.astype(jnp.float32)[:, None] * freq[None, :]
            emb = jnp.concatenate([phase, phase], axis=-1)
            return (jnp.cos(emb).astype(dtype), jnp.sin(emb).astype(dtype))

        def _rotate_half(x):
            h = x.shape[-1] // 2
            return jnp.concatenate([-x[..., h:], x[..., :h]], axis=-1)
        B, T, _ = resid.shape
        q = (resid @ Wq).reshape(B, T, N_HEADS, D_HEAD).transpose(0, 2, 1, 3)
        k = (resid @ Wk).reshape(B, T, N_KV_HEADS, D_HEAD).transpose(0, 2, 1, 3)
        v = (resid @ Wv).reshape(B, T, N_KV_HEADS, D_HEAD).transpose(0, 2, 1, 3)
        cos, sin = _rope_cos_sin(D_HEAD, jnp.arange(T), resid.dtype)
        cos = cos[None, None]
        sin = sin[None, None]
        q = q * cos + _rotate_half(q) * sin
        k = k * cos + _rotate_half(k) * sin
        qg = q.reshape(B, N_KV_HEADS, GROUP, T, D_HEAD)
        att = jnp.einsum('bhgqd,bhkd->bhgqk', qg.astype(jnp.float32), k.astype(jnp.float32)) / math.sqrt(D_HEAD)
        causal = jnp.tril(jnp.ones((T, T), dtype=bool))
        att = jnp.where(causal[None, None, None], att, -jnp.inf)
        probs = jax.nn.softmax(att, axis=-1).astype(resid.dtype)
        ctx = jnp.einsum('bhgqk,bhkd->bhgqd', probs, v)
        out = ctx.reshape(B, N_HEADS, T, D_HEAD).transpose(0, 2, 1, 3).reshape(B, T, D_MODEL)
        return out @ Wo

    def _L0_ffn_ref(x, W_gate, W_up, W_down):
        import jax, jax.numpy as jnp
        import numpy as np
        D = 512
        F = 1376
        B, S = (4, 256)
        out_shape = x.shape[:-1] + (W_down.shape[0],)
        xt = x.reshape(-1, x.shape[-1])
        up = xt @ W_up.T
        gate = jax.nn.silu(xt @ W_gate.T)
        y = gate * up @ W_down.T
        return y.reshape(out_shape)
    x = L0_attn_resid
    x = x + _L0_attn_ref(_layernorm(x, axis=-1), L0_attn_Wq, L0_attn_Wk, L0_attn_Wv, L0_attn_Wo)
    x = x + _L0_ffn_ref(_layernorm(x, axis=-1), L0_ffn_W_gate, L0_ffn_W_up, L0_ffn_W_down)
    return x

_drawn_inputs = setup_inputs


def setup_inputs(seed=0):
    import zlib

    import numpy as np

    out = dict(_drawn_inputs(seed))
    spreads = {}
    factors = {'L0_attn_Wq': 8.0, 'L0_attn_Wk': 8.0}
    for name, (base, spread) in spreads.items():
        noise = np.random.default_rng([zlib.crc32(name.encode()), seed]).standard_normal(out[name].shape)
        drawn = base * np.exp(spread * noise) if base else spread * noise
        out[name] = jnp.asarray(drawn.astype(out[name].dtype))
    for name, factor in factors.items():
        out[name] = (out[name] * factor).astype(out[name].dtype)
    return out
```

```python
from contextlib import ExitStack

import concourse.bass as bass
from concourse import mybir

F32 = mybir.dt.float32
F32R = mybir.dt.float32r
BF16 = mybir.dt.bfloat16
AXIS = mybir.AxisListType
ALU = mybir.AluOpType
ACT = mybir.ActivationFunctionType

P = 128
B, T, D = 4, 512, 512
NKV, GROUP, DH = 8, 4, 16
F = 1376
TT, KC = T // P, D // P
QT = D // P
KVW = NKV * DH
FT = -(-F // P)
FW = [min(P, F - P * f) for f in range(FT)]
SCALE = float(DH) ** -0.5
EPS = 1e-5
MASKED = -1.0e30
SCORES = TT * GROUP
HEADS_MAX = [2 if 2 * P * (q + 1) <= T else 1 for q in range(TT)]
MAX_AT = [sum(GROUP // h for h in HEADS_MAX[:q]) for q in range(TT + 1)]
MAXIMA = MAX_AT[TT]
ROWS = 3 * DH
ROWS_M = ROWS + 2
HALF = 64
RING = 4
CHUNK_N = [T - P * c for c in range(TT)]
CHUNK_AT = [sum(CHUNK_N[:c]) for c in range(TT + 1)]
DMA = 16

LN_SLOT = 4
UNIT_SLOT = {9: ("T", 0), 10: ("T", 1), 11: ("T", 2), 13: ("T", 3), 14: ("R", 0), 15: ("R", 1),
             17: ("R", 2), 18: ("R", 3), 19: ("R", 4), 21: ("V", 0)}
N_ROPE = 1 + QT


def unit_numbers(slots):
    number, n = {}, 0
    for s in range(TT * NKV):
        if s % TT == 0:
            number[s] = n
            n += 1
        elif s in slots:
            number[s] = n
            n += 1
    return number, n


UNIT_NO, UNITS = unit_numbers(UNIT_SLOT)
PRE_UNITS = KC + N_ROPE + 1 + 1


def phase_1(nc, d):
    with ExitStack() as ctx:
        def sb(name, shape, dt=F32):
            return ctx.enter_context(nc.sbuf_tensor(name, shape, dt))

        def psum(name, shape):
            return ctx.enter_context(nc.psum_tensor(name, shape, F32))

        def sem(name):
            return ctx.enter_context(nc.semaphore(name))

        ident = sb("ident", [P, P])
        ident_b = sb("ident_b", [P, P], BF16)
        mask_q = sb("mask_q", [P, P], BF16)
        mask_k = sb("mask_k", [P, P], BF16)
        minus_one = sb("minus_one", [2, T])
        half = sb("half", [P, TT])
        eps = sb("eps", [P, TT])
        cos = sb("cos", [P, T])
        sin = sb("sin", [P, T])
        w_raw = sb("w_raw", [P, KC, D + 2 * KVW])
        w_hi = sb("w_hi", [P, KC, D + 2 * KVW], F32R)
        w_lo = sb("w_lo", [P, KC, D + 2 * KVW], F32R)
        x_in = sb("x_in", [P, TT, D])
        stats = sb("stats", [P, TT, 6])
        mean_var = sb("mean_var", [P, TT, 2])
        var_eps = sb("var_eps", [P, TT])
        rstd = sb("rstd", [P, TT])
        xn = sb("xn", [P, TT, D])
        xt_hi = sb("xt_hi", [P, KC, T], F32R)
        xt_lo = sb("xt_lo", [P, KC, T], F32R)
        rot_c = sb("rot_c", [P, 2, T])
        rot_s = sb("rot_s", [P, 2, T])
        r_hi = sb("r_hi", [P, 2, T], F32R)
        r_lo = sb("r_lo", [P, 2, T], F32R)
        v_next = sb("v_next", [P, TT, KVW])
        v_ones = sb("v_ones", [P, TT, NKV, 2 * DH])
        q_rows = [sb(f"q_rows{r}", [P, GROUP // 2, T]) for r in range(RING)]
        k_rows = [sb(f"k_rows{r}", [P, T]) for r in range(RING)]
        m_raw = sb("m_raw", [P, 2, SCORES])
        m_parts = sb("m_parts", [P, 2, TT, GROUP, 2])
        m_t = [sb(f"m_t{r}", [2 * GROUP, T]) for r in range(2)]
        probs = sb("probs", [P, 2, GROUP, CHUNK_AT[TT]])
        o_sb = sb("o_sb", [P, 2, T])

        ps_s = psum("ps_s", [P, 2, T])
        ps_t = psum("ps_t", [P, GROUP, T])
        ps_o = psum("ps_o", [P, T])
        ps_d = psum("ps_d", [P, T])

        consts_ready = sem("consts_ready")
        const_step = sem("const_step")
        ones_staged = sem("ones_staged")
        tables_loaded = sem("tables_loaded")
        w_loaded = sem("w_loaded")
        w_hi_ready = sem("w_hi_ready")
        w_split = sem("w_split")
        raw_copied = sem("raw_copied")
        x_loaded = sem("x_loaded")
        ln_stats = sem("ln_stats")
        ln_mean = sem("ln_mean")
        var_ready = sem("var_ready")
        rstd_ready = sem("rstd_ready")
        xn_ready = sem("xn_ready")
        dense_ready = sem("dense_ready")
        dense_evacuated = sem("dense_evacuated")
        xt_hi_ready = sem("xt_hi_ready")
        rope_sin = sem("rope_sin")
        rope_done = sem("rope_done")
        r_hi_ready = sem("r_hi_ready")
        r_lo_ready = sem("r_lo_ready")
        r_stored = [sem(f"r_stored{k}") for k in range(N_ROPE)]
        v_ready = sem("v_ready")
        rows_staged = [sem(f"rows_staged{r}") for r in range(RING)]
        scores_ready = sem("scores_ready")
        max_done = sem("max_done")
        m_hi_ready = sem("m_hi_ready")
        m_split = sem("m_split")
        m_staged = [sem(f"m_staged{r}") for r in range(2)]
        scores_t_ready = sem("scores_t_ready")
        exp_done = sem("exp_done")
        pv_done = sem("pv_done")
        o_evacuated = sem("o_evacuated")
        o_stored = [sem(f"o_stored{r}") for r in range(2)]

        R_STORE = 2 * DMA
        ROW_DMAS = 2 * 2 * 3 * DMA
        M_DMAS = GROUP * DMA
        O_DMAS = 2 * GROUP * DMA

        block = ctx.enter_context(nc.Block())

        @block.sync
        def _(sp):
            sp.dma_start(x_in[:], d["x"][0].rearrange("(t p) n -> p t n", p=P)).then_inc(x_loaded, DMA)
            for at, name, width in ((0, "wq", D), (D, "wk", KVW), (D + KVW, "wv", KVW)):
                sp.dma_start(w_raw[:, :, at:at + width],
                             d[name].rearrange("(c p) n -> p c n", p=P)).then_inc(w_loaded, DMA)
            sp.dma_start(cos[:], d["cos"]).then_inc(tables_loaded, DMA)
            sp.dma_start(sin[:], d["sin"]).then_inc(tables_loaded, DMA)
            sp.wait_ge(consts_ready, 1)
            for r in range(RING):
                for s in range(2):
                    at = HALF * s + ROWS
                    sp.dma_start(k_rows[r][at:at + 2, :], minus_one[:]).then_inc(ones_staged, DMA)

            def store_rotated(b, k):
                sp.wait_ge(r_lo_ready, N_ROPE * b + k + 1)
                for part, tile in ((0, r_hi), (1, r_lo)):
                    to = d["k_parts"][b, part] if k == 0 else d["q_parts"][b, part, P * (k - 1):P * k]
                    sp.dma_start(to, tile[:, k % 2, :].bitcast(F32)).then_inc(r_stored[k], DMA)

            def stage_rows(b, g, n):
                used = SCORES * (n - RING + 1)
                sp.compute_val(used)
                if g == 0:
                    sp.wait_ge(r_stored[0], R_STORE * (b + 1))
                if g % 2 == 0:
                    sp.wait_ge(r_stored[1 + g // 2], R_STORE * (b + 1))
                if not isinstance(n, int) or n >= RING:
                    sp.wait_ge(scores_t_ready, used)
                r = g % RING
                for s in range(2):
                    for row, (q_part, k_part) in enumerate(((0, 0), (0, 1), (1, 0))):
                        at = HALF * s + DH * row
                        heads = d["q_parts"][b, q_part, HALF * g:HALF * (g + 1)]
                        heads = heads.rearrange("(i s w) t -> s w i t", s=2, w=DH)[s]
                        sp.dma_start(q_rows[r][at:at + DH], heads).then_inc(rows_staged[r], DMA)
                        sp.dma_start(k_rows[r][at:at + DH, :],
                                     d["k_parts"][b, k_part, DH * g:DH * (g + 1)]).then_inc(rows_staged[r], DMA)

            def stage_max(g, unit):
                sp.wait_ge(dense_evacuated, unit + 1)
                r = g % RING
                for j in range(GROUP):
                    at = HALF * (j % 2) + ROWS
                    sp.dma_start(q_rows[r][at:at + 2, j // 2, :],
                                 m_t[g % 2][2 * j:2 * j + 2, :]).then_inc(m_staged[g % 2], DMA)

            def store_o(b, g):
                sp.wait_ge(o_evacuated, NKV * b + g + 1)
                for j in range(GROUP):
                    at = DH * (GROUP * g + j)
                    sp.dma_start(d["o"][b, at:at + DH], o_sb[32 * j:32 * j + DH, g % 2, :]).then_inc(o_stored[g % 2], DMA)
                    sp.dma_start(d["sums"][b, at:at + DH],
                                 o_sb[32 * j + DH:32 * j + 2 * DH, g % 2, :]).then_inc(o_stored[g % 2], DMA)

            def iteration(b, has_next):
                if has_next:
                    sp.wait_ge(xn_ready, TT * (b + 1))
                    sp.dma_start(x_in[:], d["x"][b + 1].rearrange("(t p) n -> p t n", p=P)).then_inc(x_loaded, DMA)
                for slot in range(TT * NKV):
                    g, i = slot // TT, slot % TT
                    unit0 = UNITS * b + PRE_UNITS
                    if i == 1 and (has_next or g < NKV - 1):
                        stage_max(g + 1, unit0 + (UNIT_NO[slot - 1] if has_next else g))
                    if i == 1 and g >= 1:
                        store_o(b, g - 1)
                    if has_next and UNIT_SLOT.get(slot - 3, "-")[0] == "R":
                        store_rotated(b + 1, UNIT_SLOT[slot - 3][1])
                    if i == 2 and g + 3 < NKV:
                        stage_rows(b, g + 3, NKV * b + g + 3)
                    if i == 2 and g + 3 >= NKV and has_next:
                        stage_rows(b + 1, g + 3 - NKV, NKV * b + g + 3)
                store_o(b, NKV - 1)

            for k in range(N_ROPE):
                store_rotated(0, k)
                if k in (1, 2):
                    for g in range(2 * (k - 1), min(2 * k, 3)):
                        stage_rows(0, g, g)
            stage_max(0, PRE_UNITS - 1)
            for name in ("wo", "wg", "wu", "wd"):
                sp.dma_start(d[name + "_raw"], d[name]).then_inc(raw_copied, DMA)
            with sp.Fori(0, B - 1) as b:
                iteration(b, True)
            iteration(B - 1, False)
            for stored in o_stored:
                sp.wait_ge(stored, O_DMAS * NKV // 2 * B)
            sp.wait_ge(raw_copied, 4 * DMA)
            for stored in r_stored:
                sp.wait_ge(stored, R_STORE * B)

        @block.gpsimd
        def _(pool):
            pool.memset(half[:], -0.5)
            pool.memset(eps[:], EPS)
            pool.memset(minus_one[:], -1.0)
            pool.memset(v_ones[:], 1.0)
            pool.memset(ident[:], 0.0)
            pool.memset(ident_b[:], 0.0)
            pool.memset(mask_q[:], 0.0)
            pool.memset(mask_k[:], 0.0).then_inc(const_step, 1)
            pool.wait_ge(const_step, 1)
            for tile in (ident, ident_b):
                nc.gpsimd.affine_select(out=tile[:], in_=tile[:], compare_op=ALU.not_equal, fill=1.0, base=0,
                                        pattern=[[-1, P]], channel_multiplier=1)
            nc.gpsimd.affine_select(out=mask_q[:], in_=mask_q[:], compare_op=ALU.is_ge, fill=MASKED, base=0,
                                    pattern=[[-1, P]], channel_multiplier=1)
            nc.gpsimd.affine_select(out=mask_k[:], in_=mask_k[:], compare_op=ALU.is_ge, fill=MASKED, base=0,
                                    pattern=[[1, P]], channel_multiplier=-1).then_inc(consts_ready, 1)
            pool.wait_ge(consts_ready, 1)

            def layernorm_scale(b):
                pool.wait_ge(ln_mean, TT * (b + 1))
                nc.gpsimd.tensor_tensor(var_eps[:], mean_var[:, :, 1], eps[:], ALU.add).then_inc(var_ready, 1)
                pool.wait_ge(var_ready, b + 1)
                nc.gpsimd.tensor_tensor(rstd[:], var_eps[:], half[:], ALU.pow).then_inc(rstd_ready, 1)

            def rotate(b, k, unit):
                r = k % 2
                pool.wait_ge(dense_evacuated, unit + 1)
                nc.gpsimd.tensor_tensor(rot_s[:, r], rot_s[:, r], sin[:], ALU.mult).then_inc(rope_sin, 1)
                pool.wait_ge(rope_sin, N_ROPE * b + k + 1)
                nc.gpsimd.tensor_tensor(rot_c[:, r], rot_c[:, r], rot_s[:, r], ALU.add).then_inc(rope_done, 1)

            pool.wait_ge(tables_loaded, 2 * DMA)
            layernorm_scale(0)
            for k in range(N_ROPE):
                rotate(0, k, KC + k)
            with pool.Fori(0, B - 1) as b:
                layernorm_scale(b + 1)
                for slot, (kind, k) in UNIT_SLOT.items():
                    if kind == "R":
                        rotate(b + 1, k, UNITS * b + PRE_UNITS + UNIT_NO[slot])

        @block.scalar
        def _(act):
            def xt_high(unit, kc):
                act.wait_ge(dense_ready, unit + 1)
                nc.scalar.copy(xt_hi[:, kc], ps_d[:]).then_inc(xt_hi_ready, 1)

            def rotated_high(b, k):
                act.wait_ge(rope_done, N_ROPE * b + k + 1)
                if k >= 2:
                    act.wait_ge(r_stored[k - 2], R_STORE * (b + 1))
                elif not isinstance(b, int):
                    act.wait_ge(r_stored[N_ROPE - 1 - k], R_STORE * b)
                nc.scalar.copy(r_hi[:, k % 2], rot_c[:, k % 2]).then_inc(r_hi_ready, 1)

            def v_evacuate(unit):
                act.wait_ge(dense_ready, unit + 1)
                nc.scalar.copy(v_next[:].rearrange("p t n -> p (t n)"), ps_d[:]).then_inc(dense_evacuated, 1)

            def v_place(b, unit):
                act.wait_ge(dense_evacuated, unit + 1)
                nc.scalar.copy(v_ones[:, :, :, 0:DH].rearrange("p t h w -> p (t h) w"),
                               v_next[:].rearrange("p t (h w) -> p (t h) w", w=DH)).then_inc(v_ready, 1)

            def max_evacuate(b, g, unit):
                act.wait_ge(dense_ready, unit + 1)
                if not isinstance(b, int) or b >= 1 or g >= 2:
                    act.wait_ge(m_staged[g % 2], M_DMAS * (NKV // 2 * b + g // 2))
                nc.scalar.copy(m_t[g % 2][:], ps_d[0:2 * GROUP, :]).then_inc(dense_evacuated, 1)

            def exponentials(b, g, c):
                for j in range(GROUP):
                    n = SCORES * (NKV * b + g) + GROUP * c + j
                    if c == 0 and j == 0:
                        act.wait_ge(pv_done, NKV * b + max(g - 1, 0))
                    act.wait_ge(scores_t_ready, n + 1)
                    nc.scalar.activation(probs[:, g % 2, j, CHUNK_AT[c]:CHUNK_AT[c + 1]],
                                         ps_t[:, j, 0:CHUNK_N[c]], ACT.Exp, scale=SCALE).then_inc(exp_done, 1)

            def o_evacuate(b, g):
                act.wait_ge(pv_done, NKV * b + g + 1)
                act.wait_ge(o_stored[g % 2], O_DMAS * (NKV // 2 * b + g // 2))
                nc.scalar.copy(o_sb[:, g % 2], ps_o[:]).then_inc(o_evacuated, 1)

            def iteration(b, has_next):
                unit0 = UNITS * b + PRE_UNITS
                for slot in range(TT * NKV):
                    g, i = slot // TT, slot % TT
                    if i == 1 and (has_next or g < NKV - 1):
                        max_evacuate(b, g + 1, unit0 + (UNIT_NO[slot - 1] if has_next else g))
                    kind, k = UNIT_SLOT.get(slot - 1, "--")
                    if has_next and kind == "T":
                        xt_high(unit0 + UNIT_NO[slot - 1], k)
                    if has_next and kind == "V":
                        v_evacuate(unit0 + UNIT_NO[slot - 1])
                    if i == 1 and g >= 1:
                        o_evacuate(b, g - 1)
                    exponentials(b, g, i)
                    kind, k = UNIT_SLOT.get(slot - 2, "--")
                    if has_next and kind == "R":
                        rotated_high(b + 1, k)
                o_evacuate(b, NKV - 1)
                if has_next:
                    v_place(b, unit0 + UNIT_NO[[s for s, u in UNIT_SLOT.items() if u[0] == "V"][0]])

            act.wait_ge(w_loaded, 3 * DMA)
            for c in range(KC):
                nc.scalar.copy(w_hi[:, c], w_raw[:, c]).then_inc(w_hi_ready, 1)
            for kc in range(KC):
                xt_high(kc, kc)
            for k in range(N_ROPE):
                rotated_high(0, k)
            v_evacuate(KC + N_ROPE)
            act.wait_ge(consts_ready, 1)
            v_place(0, KC + N_ROPE)
            max_evacuate(0, 0, PRE_UNITS - 1)
            with act.Fori(0, B - 1) as b:
                iteration(b, True)
            iteration(B - 1, False)

        @block.vector
        def _(dve):
            swap = [(p + DH // 2) % DH + DH * (p // DH) for p in range(32)]

            def layernorm_stats(b):
                dve.wait_ge(x_loaded, DMA * (b + 1))
                for t in range(TT):
                    nc.vector.bn_stats(stats[:, t], x_in[:, t]).then_inc(ln_stats, 1)

            def layernorm_mean():
                for t in range(TT):
                    nc.vector.bn_aggr(mean_var[:, t], stats[:, t]).then_inc(ln_mean, 1)

            def layernorm_apply(b):
                dve.wait_ge(rstd_ready, b + 1)
                for t in range(TT):
                    nc.vector.tensor_scalar(xn[:, t], x_in[:, t], mean_var[:, t, 0:1], rstd[:, t:t + 1],
                                            ALU.subtract, ALU.mult).then_inc(xn_ready, 1)

            def xt_low(b, kc):
                dve.wait_ge(xt_hi_ready, KC * b + kc + 1)
                nc.vector.tensor_tensor(xt_lo[:, kc], ps_d[:], xt_hi[:, kc].bitcast(F32),
                                        ALU.subtract).then_inc(dense_evacuated, 1)

            def rope_parts(b, k, unit):
                r = k % 2
                if k >= 2:
                    dve.wait_ge(r_lo_ready, N_ROPE * b + k - 1)
                elif not isinstance(b, int):
                    dve.wait_ge(r_lo_ready, N_ROPE * b)
                dve.wait_ge(dense_ready, unit + 1)
                nc.vector.tensor_tensor(rot_c[:, r], ps_d[:], cos[:], ALU.mult)
                nc.vector.stream_shuffle(rot_s[:, r], ps_d[:], swap).then_inc(dense_evacuated, 1)

            def rotated_low(b, k):
                r = k % 2
                dve.wait_ge(r_hi_ready, N_ROPE * b + k + 1)
                nc.vector.tensor_tensor(r_lo[:, r], rot_c[:, r], r_hi[:, r].bitcast(F32),
                                        ALU.subtract).then_inc(r_lo_ready, 1)

            def row_max(n, g, q):
                heads = HEADS_MAX[q]
                for j in range(GROUP // heads):
                    dve.wait_ge(scores_ready, MAXIMA * n + MAX_AT[q] + j + 1)
                    nc.vector.tensor_reduce(
                        out=m_raw[:, g % 2, GROUP * q + j:GROUP * (q + 1):GROUP // heads], op=ALU.max, axis=AXIS.X,
                        in_=ps_s[:, j % 2, 0:heads * P * (q + 1)].rearrange("p (j t) -> p j t", j=heads)
                    ).then_inc(max_done, 1)

            def split_max(n, g):
                r = g % 2
                raw = m_raw[:, r, :]
                hi = m_parts[:, r, :, :, 0].rearrange("p q j -> p (q j)")
                lo = m_parts[:, r, :, :, 1].rearrange("p q j -> p (q j)")
                dve.wait_ge(max_done, MAXIMA * (n + 1))
                nc.vector.tensor_copy(hi.bitcast(F32R), raw).then_inc(m_hi_ready, 1)
                dve.wait_ge(m_hi_ready, n + 1)
                nc.vector.tensor_tensor(lo.bitcast(F32R), raw, hi, ALU.subtract).then_inc(m_split, 1)

            def iteration(b, has_next):
                unit0 = UNITS * b + PRE_UNITS
                for slot in range(TT * NKV):
                    g, i = slot // TT, slot % TT
                    kind, k = UNIT_SLOT.get(slot - 3, "--")
                    if has_next and kind == "R":
                        rotated_low(b + 1, k)
                    kind, k = UNIT_SLOT.get(slot - 1, "--")
                    if has_next and kind == "T":
                        xt_low(b + 1, k)
                    if has_next and kind == "R":
                        rope_parts(b + 1, k, unit0 + UNIT_NO[slot - 1])
                    if has_next and slot == LN_SLOT + 1:
                        dve.wait_ge(ln_stats, TT * (b + 2))
                    if has_next or g < NKV - 2:
                        row_max(NKV * b + g + 2, g, i)
                        if i == TT - 1:
                            split_max(NKV * b + g + 2, g)
                    if has_next and slot == LN_SLOT:
                        layernorm_stats(b + 1)
                    if has_next and slot == LN_SLOT + 1:
                        layernorm_mean()
                    if has_next and slot == LN_SLOT + 2:
                        layernorm_apply(b + 1)

            layernorm_stats(0)
            dve.wait_ge(ln_stats, TT)
            layernorm_mean()
            layernorm_apply(0)
            for c in range(KC):
                dve.wait_ge(w_hi_ready, c + 1)
                nc.vector.tensor_tensor(w_lo[:, c], w_raw[:, c], w_hi[:, c].bitcast(F32),
                                        ALU.subtract).then_inc(w_split, 1)
            for kc in range(KC):
                xt_low(0, kc)
            dve.wait_ge(tables_loaded, 2 * DMA)
            for k in range(N_ROPE):
                if k >= 2:
                    rotated_low(0, k - 2)
                rope_parts(0, k, KC + k)
            rotated_low(0, N_ROPE - 2)
            rotated_low(0, N_ROPE - 1)
            dve.wait_ge(consts_ready, 1)
            for g in range(2):
                for q in range(TT):
                    row_max(g, g, q)
                split_max(g, g)
            with dve.Fori(0, B - 1) as b:
                iteration(b, True)
            iteration(B - 1, False)

        @block.tensor
        def _(pe):
            def bank_free(unit):
                if not isinstance(unit, int) or unit > 0:
                    pe.wait_ge(dense_evacuated, unit)

            def transposed_x(b, kc, unit):
                pe.wait_ge(xn_ready, TT * (b + 1))
                bank_free(unit)
                for t in range(TT):
                    mm = nc.tensor.transpose(ps_d[:, P * t:P * (t + 1)], xn[:, t, P * kc:P * (kc + 1)], ident[:])
                mm.then_inc(dense_ready, 1)

            def three_products(out, weights, moving):
                for c in range(KC):
                    for n, (w, m) in enumerate(((0, 0), (0, 1), (1, 0))):
                        mm = nc.tensor.matmul(out, weights(w, c), moving(m, c), start=(c == 0 and n == 0),
                                              stop=(c == KC - 1 and n == 2))
                return mm

            W, X = (w_hi, w_lo), (xt_hi, xt_lo)

            def project(k, unit):
                at = D if k == 0 else P * (k - 1)
                bank_free(unit)
                three_products(ps_d[:], lambda w, c: W[w][:, c, at:at + P], lambda m, c: X[m][:, c, :]
                               ).then_inc(dense_ready, 1)

            def project_v(unit):
                bank_free(unit)
                for t in range(TT):
                    mm = three_products(ps_d[:, KVW * t:KVW * (t + 1)], lambda w, c: X[w][:, c, P * t:P * (t + 1)],
                                        lambda m, c: W[m][:, c, D + KVW:D + 2 * KVW])
                mm.then_inc(dense_ready, 1)

            def scores(b, g, q, j):
                n = NKV * b + g
                r, at = g % RING, HALF * (j % 2)
                heads, width = HEADS_MAX[q], P * (q + 1)
                unit, place = MAX_AT[q] + j % (GROUP // heads), j // (GROUP // heads)
                if q == 0 and j == 0:
                    pe.wait_ge(rows_staged[r], ROW_DMAS * (NKV // RING * b + g // RING + 1))
                k = MAXIMA * n + unit
                if place == 0 and (not isinstance(k, int) or k >= 2):
                    pe.wait_ge(max_done, k - 1)
                out = ps_s[:, j % 2, width * place:width * (place + 1)]
                nc.tensor.matmul(out, q_rows[r][at:at + ROWS, j // 2, P * q:P * (q + 1)].bitcast(F32R),
                                 k_rows[r][at:at + ROWS, 0:width].bitcast(F32R), start=True, stop=False)
                mm = nc.tensor.matmul(out[:, P * q:width], ident_b[:], mask_q[:], start=False, stop=True)
                if place == heads - 1:
                    mm.then_inc(scores_ready, 1)

            def transposed_max(n, g, unit):
                pe.wait_ge(m_split, n + 1)
                bank_free(unit)
                for q in range(TT):
                    mm = nc.tensor.transpose(ps_d[0:2 * GROUP, P * q:P * (q + 1)],
                                             m_parts[:, g % 2, q].rearrange("p j w -> p (j w)"), ident[:])
                mm.then_inc(dense_ready, 1)

            def scores_t(b, g, c, j):
                n = NKV * b + g
                r, at = g % RING, HALF * (j % 2)
                if c == 0 and j == 0:
                    pe.wait_ge(m_staged[g % 2], M_DMAS * (NKV // 2 * b + g // 2 + 1))
                if g == 0 and c == 0:
                    pe.wait_ge(exp_done, SCORES * n)
                else:
                    pe.wait_ge(exp_done, SCORES * n + GROUP * c + j - GROUP + 1)
                out = ps_t[:, j, 0:CHUNK_N[c]]
                nc.tensor.matmul(out, k_rows[r][at:at + ROWS_M, P * c:P * (c + 1)].bitcast(F32R),
                                 q_rows[r][at:at + ROWS_M, j // 2, P * c:T].bitcast(F32R), start=True, stop=False)
                nc.tensor.matmul(ps_t[:, j, 0:P], ident_b[:], mask_k[:], start=False,
                                 stop=True).then_inc(scores_t_ready, 1)

            def weighted_v(b, g, c):
                n = NKV * b + g
                pe.wait_ge(exp_done, SCORES * n + GROUP * (c + 1))
                if c == 0:
                    pe.wait_ge(o_evacuated, n)
                    if g == 0:
                        pe.wait_ge(v_ready, b + 1)
                for j in range(GROUP):
                    mm = nc.tensor.matmul(ps_o[32 * j:32 * j + 2 * DH, P * c:T], v_ones[:, c, g, :],
                                          probs[:, g % 2, j, CHUNK_AT[c]:CHUNK_AT[c + 1]],
                                          start=(c == 0), stop=(c == TT - 1))
                if c == TT - 1:
                    mm.then_inc(pv_done, 1)

            def iteration(b, has_next):
                unit0 = UNITS * b + PRE_UNITS
                for slot in range(TT * NKV):
                    g, i = slot // TT, slot % TT
                    for j in range(GROUP):
                        if has_next or g < NKV - 2:
                            scores(b, g + 2, i, j)
                        scores_t(b, g, i, j)
                    if i >= 1:
                        weighted_v(b, g, i - 1)
                    elif g >= 1:
                        weighted_v(b, g - 1, TT - 1)
                    if i == 0 and (has_next or g < NKV - 1):
                        transposed_max(NKV * b + g + 1, g + 1, unit0 + (UNIT_NO[slot] if has_next else g))
                    kind, k = UNIT_SLOT.get(slot, "--")
                    if has_next and kind == "T":
                        transposed_x(b + 1, k, unit0 + UNIT_NO[slot])
                    if has_next and kind == "R":
                        project(k, unit0 + UNIT_NO[slot])
                    if has_next and kind == "V":
                        project_v(unit0 + UNIT_NO[slot])
                weighted_v(b, NKV - 1, TT - 1)

            pe.wait_ge(consts_ready, 1)
            for kc in range(KC):
                transposed_x(0, kc, kc)
            pe.wait_ge(w_split, KC)
            for k in range(N_ROPE):
                project(k, KC + k)
            project_v(KC + N_ROPE)
            pe.wait_ge(ones_staged, 2 * RING * DMA)
            for g in range(2):
                for q in range(TT):
                    for j in range(GROUP):
                        scores(0, g, q, j)
            transposed_max(0, 0, PRE_UNITS - 1)
            with pe.Fori(0, B - 1) as b:
                iteration(b, True)
            iteration(B - 1, False)


WO_SLOT = 3


def ring_units(has_next):
    units = []
    for f in range(FT):
        units += [("gate", f), ("up", f)]
        if has_next and 0 <= f - WO_SLOT < TT:
            units.append(("wo", f - WO_SLOT))
    if has_next:
        units += [("T", kc) for kc in range(KC)]
    return {u: n for n, u in enumerate(units)}


BANKS = 4
RING_PRE = {u: n for n, u in enumerate([("wo", t) for t in range(TT)] + [("T", c) for c in range(KC)])}
RING_FULL = ring_units(True)
RING_LAST = ring_units(False)
assert len(RING_PRE) % BANKS == 0


def phase_2(nc, d):
    with ExitStack() as ctx:
        def sb(name, shape, dt=F32):
            return ctx.enter_context(nc.sbuf_tensor(name, shape, dt))

        def sem(name):
            return ctx.enter_context(nc.semaphore(name))

        wo = [sb(f"wo_{p}", [P, KC, D], F32R) for p in ("hi", "lo")]
        wg = [sb(f"wg_{p}", [P, KC, F], F32R) for p in ("hi", "lo")]
        wu = [sb(f"wu_{p}", [P, KC, F], F32R) for p in ("hi", "lo")]
        wd = [sb(f"wd_{p}", [P, FT, D], F32R) for p in ("hi", "lo")]
        ident = sb("ident2", [P, P])
        half = sb("half2", [P, 1])
        eps = sb("eps2", [P, 1])
        o_in = sb("o_in", [P, QT, P])
        sums = sb("sums_in", [P, QT, P])
        ctx_t = [sb(f"ctx_{p}", [P, QT, P], F32R) for p in ("hi", "lo")]
        x_res = sb("x_res", [P, 2, D])
        xn = sb("xn2", [P, TT, D])
        y = sb("y", [P, TT, D])
        stats = sb("stats2", [P, 6])
        mean_var = sb("mean_var2", [P, 2])
        var_eps = sb("var_eps2", [P, 1])
        rstd = sb("rstd2", [P, 1])
        xt = [sb(f"x2t_{p}", [P, KC, T], F32R) for p in ("hi", "lo")]
        h = sb("h", [P, 2, T])
        h_parts = [sb(f"h_{p}", [P, 2, T], F32R) for p in ("hi", "lo")]
        bank = [ctx.enter_context(nc.psum_tensor(f"bank{k}", [P, T], F32)) for k in range(BANKS)]
        ps_y = ctx.enter_context(nc.psum_tensor("ps_y", [P, TT, D], F32))

        ident_step = sem("ident_step")
        ident_ready = sem("ident_ready")
        wo_loaded = sem("wo_loaded")
        wo_hi_ready = sem("wo_hi_ready")
        wo_split = sem("wo_split")
        ffn_loaded = [sem(f"ffn_loaded{f}") for f in range(FT)]
        ffn_hi_ready = sem("ffn_hi_ready")
        ffn_split = sem("ffn_split")
        o_loaded = sem("o_loaded")
        xres_loaded = [sem(f"xres_loaded{r}") for r in range(2)]
        recip_done = sem("recip_done")
        ctx_scaled = sem("ctx_scaled")
        ctx_hi_ready = sem("ctx_hi_ready")
        ctx_lo_ready = sem("ctx_lo_ready")
        wo_done = sem("wo_done")
        x1_ready = sem("x1_ready")
        x1_stored = sem("x1_stored")
        ln_stats = sem("ln2_stats")
        ln_mean = sem("ln2_mean")
        var_ready = sem("var2_ready")
        rstd_ready = sem("rstd2_ready")
        xn_ready = sem("xn2_ready")
        xt_done = sem("x2t_done")
        xt_hi_ready = sem("x2t_hi_ready")
        xt_ready = sem("x2t_ready")
        gate_ready = sem("gate_ready")
        up_ready = sem("up_ready")
        silu_done = sem("silu_done")
        h_ready = sem("h_ready")
        h_hi_ready = sem("h_hi_ready")
        h_lo_ready = sem("h_lo_ready")
        down_done = sem("down_done")
        y_loaded = sem("y_loaded")
        y_evacuated = sem("y_evacuated")
        y_stored = sem("y_stored")

        W_DMAS = 3 * DMA

        block = ctx.enter_context(nc.Block())

        @block.sync
        def _(sp):
            def load_o(b, t):
                n = TT * b + t
                if not isinstance(n, int) or n >= 1:
                    sp.wait_ge(ctx_lo_ready, n)
                for tile, name in ((o_in, "o"), (sums, "sums")):
                    sp.dma_start(tile[:], d[name][b].rearrange("(c p) t -> p c t", p=P)[:, :, P * t:P * (t + 1)]
                                 ).then_inc(o_loaded, DMA)

            def load_residual(b, t):
                n = TT * b + t
                if not isinstance(n, int) or n >= 2:
                    sp.wait_ge(x1_ready, n - 1)
                sp.dma_start(x_res[:, t % 2], d["x"][b, P * t:P * (t + 1)]).then_inc(xres_loaded[t % 2], DMA)

            def store_x1(b, t):
                sp.wait_ge(x1_ready, TT * b + t + 1)
                sp.dma_start(d["x1"][b, P * t:P * (t + 1)], xn[:, t]).then_inc(x1_stored, DMA)

            def iteration(b, has_next):
                if not isinstance(b, int) or b > 0:
                    sp.wait_ge(y_stored, TT * DMA * b)
                sp.wait_ge(x1_stored, TT * DMA * (b + 1))
                sp.dma_start(y[:], d["x1"][b].rearrange("(t p) n -> p t n", p=P)).then_inc(y_loaded, DMA)
                if has_next:
                    for t in range(2):
                        load_o(b + 1, t)
                        load_residual(b + 1, t)
                    for t in range(TT):
                        if t + 2 < TT:
                            load_o(b + 1, t + 2)
                        store_x1(b + 1, t)
                        if t + 2 < TT:
                            load_residual(b + 1, t + 2)
                for t in range(TT):
                    sp.wait_ge(y_evacuated, TT * b + t + 1)
                    sp.dma_start(d["out"][b, P * t:P * (t + 1)], y[:, t]).then_inc(y_stored, DMA)

            load_o(0, 0)
            load_residual(0, 0)
            sp.dma_start(wo[1][:].bitcast(F32), d["wo_raw"].rearrange("(c p) n -> p c n", p=P)
                         ).then_inc(wo_loaded, DMA)
            for f in range(FT):
                m = FW[f]
                for w, name in ((wg, "wg_raw"), (wu, "wu_raw")):
                    sp.dma_start(w[1][:, :, P * f:P * f + m].bitcast(F32),
                                 d[name].rearrange("(c p) n -> p c n", p=P)[:, :, P * f:P * f + m]
                                 ).then_inc(ffn_loaded[f], DMA)
                sp.dma_start(wd[1][0:m, f].bitcast(F32), d["wd_raw"][P * f:P * f + m]).then_inc(ffn_loaded[f], DMA)
                if f < TT:
                    if f + 1 < TT:
                        load_o(0, f + 1)
                        load_residual(0, f + 1)
                    store_x1(0, f)
            iteration(0, True)
            with sp.Fori(1, B - 1) as b:
                iteration(b, True)
            iteration(B - 1, False)
            sp.wait_ge(y_stored, TT * DMA * B)
            sp.wait_ge(x1_stored, TT * DMA * B)

        @block.gpsimd
        def _(pool):
            pool.memset(half[:], -0.5)
            pool.memset(eps[:], EPS)
            pool.memset(ident[:], 0.0).then_inc(ident_step, 1)
            pool.wait_ge(ident_step, 1)
            nc.gpsimd.affine_select(out=ident[:], in_=ident[:], compare_op=ALU.not_equal, fill=1.0, base=0,
                                    pattern=[[-1, P]], channel_multiplier=1).then_inc(ident_ready, 1)
            pool.wait_ge(ident_ready, 1)
            with pool.Fori(0, B * TT) as n:
                pool.wait_ge(ln_mean, n + 1)
                nc.gpsimd.tensor_tensor(var_eps[:], mean_var[:, 1:2], eps[:], ALU.add).then_inc(var_ready, 1)
                pool.wait_ge(var_ready, n + 1)
                nc.gpsimd.tensor_tensor(rstd[:], var_eps[:], half[:], ALU.pow).then_inc(rstd_ready, 1)

        @block.scalar
        def _(act):
            def split_ffn_hi(f):
                act.wait_ge(ffn_loaded[f], W_DMAS)
                m = FW[f]
                for w in (wg, wu):
                    nc.scalar.copy(w[0][:, :, P * f:P * f + m], w[1][:, :, P * f:P * f + m].bitcast(F32)
                                   ).then_inc(ffn_hi_ready, 1)
                nc.scalar.copy(wd[0][0:m, f], wd[1][0:m, f].bitcast(F32)).then_inc(ffn_hi_ready, 1)

            def ctx_hi(n):
                act.wait_ge(ctx_scaled, n + 1)
                if not isinstance(n, int) or n >= 1:
                    act.wait_ge(wo_done, n)
                nc.scalar.copy(ctx_t[0][:], o_in[:]).then_inc(ctx_hi_ready, 1)

            def xt_hi(b, kc, units):
                act.wait_ge(xt_done, KC * b + kc + 1)
                nc.scalar.copy(xt[0][:, kc], bank[units["T", kc] % BANKS][:]).then_inc(xt_hi_ready, 1)

            def iteration(b, has_next):
                units = RING_FULL if has_next else RING_LAST
                first = isinstance(b, int) and b == 0
                for f in range(FT):
                    n, m, r = FT * b + f, FW[f], f % 2
                    act.wait_ge(gate_ready, n + 1)
                    if not first or f >= 2:
                        act.wait_ge(h_lo_ready, FT * b if f < 2 else n - 1)
                    nc.scalar.activation(h[0:m, r], bank[units["gate", f] % BANKS][0:m, :], ACT.Silu
                                         ).then_inc(silu_done, 1)
                    act.wait_ge(h_ready, n + 1)
                    if not first or f >= 2:
                        act.wait_ge(down_done, FT * b if f < 2 else n - 1)
                    nc.scalar.copy(h_parts[0][0:m, r], h[0:m, r]).then_inc(h_hi_ready, 1)
                    if first and f + 2 < FT:
                        split_ffn_hi(f + 2)
                    if has_next and 0 <= f - WO_SLOT + 1 < TT:
                        ctx_hi(TT * (b + 1) + f - WO_SLOT + 1)
                if has_next:
                    for kc in range(KC):
                        xt_hi(b + 1, kc, units)

            act.wait_ge(wo_loaded, DMA)
            for c in range(KC):
                nc.scalar.copy(wo[0][:, c], wo[1][:, c].bitcast(F32)).then_inc(wo_hi_ready, 1)
            ctx_hi(0)
            split_ffn_hi(0)
            ctx_hi(1)
            split_ffn_hi(1)
            ctx_hi(2)
            ctx_hi(3)
            for kc in range(KC):
                xt_hi(0, kc, RING_PRE)
            iteration(0, True)
            with act.Fori(1, B - 1) as b:
                iteration(b, True)
            iteration(B - 1, False)

        @block.vector
        def _(dve):
            def split_ffn_lo(f):
                m = FW[f]
                for k, w in enumerate((wg, wu)):
                    at = P * f
                    dve.wait_ge(ffn_hi_ready, 3 * f + k + 1)
                    nc.vector.tensor_tensor(w[1][:, :, at:at + m], w[1][:, :, at:at + m].bitcast(F32),
                                            w[0][:, :, at:at + m].bitcast(F32), ALU.subtract).then_inc(ffn_split, 1)
                dve.wait_ge(ffn_hi_ready, 3 * f + 3)
                nc.vector.tensor_tensor(wd[1][0:m, f], wd[1][0:m, f].bitcast(F32), wd[0][0:m, f].bitcast(F32),
                                        ALU.subtract).then_inc(ffn_split, 1)

            def scale_ctx(n):
                dve.wait_ge(o_loaded, 2 * DMA * (n + 1))
                nc.vector.reciprocal(sums[:], sums[:]).then_inc(recip_done, 1)
                dve.wait_ge(recip_done, n + 1)
                nc.vector.tensor_tensor(o_in[:], o_in[:], sums[:], ALU.mult).then_inc(ctx_scaled, 1)

            def ctx_lo(n):
                dve.wait_ge(ctx_hi_ready, n + 1)
                nc.vector.tensor_tensor(ctx_t[1][:], o_in[:], ctx_t[0][:].bitcast(F32),
                                        ALU.subtract).then_inc(ctx_lo_ready, 1)

            def residual(b, t, units):
                n = TT * b + t
                dve.wait_ge(wo_done, n + 1)
                dve.wait_ge(xres_loaded[t % 2], DMA * (TT // 2 * b + t // 2 + 1))
                k = units["wo", t] % BANKS
                nc.vector.tensor_tensor(xn[:, t], bank[k][:], x_res[:, t % 2], ALU.add
                                        ).then_inc(x1_ready, 1)
                dve.wait_ge(x1_ready, n + 1)
                nc.vector.bn_stats(stats[:], xn[:, t]).then_inc(ln_stats, 1)

            def mean():
                nc.vector.bn_aggr(mean_var[:], stats[:]).then_inc(ln_mean, 1)

            def normalise(n, t):
                dve.wait_ge(rstd_ready, n + 1)
                dve.wait_ge(x1_stored, DMA * (n + 1))
                nc.vector.tensor_scalar(xn[:, t], xn[:, t], mean_var[:, 0:1], rstd[:, 0:1], ALU.subtract,
                                        ALU.mult).then_inc(xn_ready, 1)

            def xt_lo(b, kc, units):
                k = units["T", kc] % BANKS
                dve.wait_ge(xt_hi_ready, KC * b + kc + 1)
                nc.vector.tensor_tensor(xt[1][:, kc], bank[k][:], xt[0][:, kc].bitcast(F32),
                                        ALU.subtract).then_inc(xt_ready, 1)

            def iteration(b, has_next):
                units = RING_FULL if has_next else RING_LAST
                first = isinstance(b, int) and b == 0
                for f in range(FT):
                    n, m, r = FT * b + f, FW[f], f % 2
                    stats_of = f - WO_SLOT - 2
                    normalised = has_next and 0 <= stats_of < TT
                    if normalised:
                        dve.wait_ge(ln_stats, TT * (b + 1) + stats_of + 1)
                    dve.wait_ge(silu_done, n + 1)
                    dve.wait_ge(up_ready, n + 1)
                    nc.vector.tensor_tensor(h[0:m, r], h[0:m, r], bank[units["up", f] % BANKS][0:m, :],
                                            ALU.mult).then_inc(h_ready, 1)
                    if normalised:
                        mean()
                    dve.wait_ge(h_hi_ready, n + 1)
                    nc.vector.tensor_tensor(h_parts[1][0:m, r], h[0:m, r], h_parts[0][0:m, r].bitcast(F32),
                                            ALU.subtract).then_inc(h_lo_ready, 1)
                    if first and f + 2 < FT:
                        split_ffn_lo(f + 2)
                    if has_next:
                        t = f - WO_SLOT + 1
                        if 0 <= t < TT:
                            scale_ctx(TT * (b + 1) + t)
                            ctx_lo(TT * (b + 1) + t)
                        if normalised:
                            normalise(TT * (b + 1) + stats_of, stats_of)
                        if 0 <= t - 2 < TT:
                            residual(b + 1, t - 2, units)
                if has_next:
                    for kc in range(KC):
                        xt_lo(b + 1, kc, units)
                dve.wait_ge(y_loaded, DMA * (b + 1))
                dve.wait_ge(down_done, FT * (b + 1))
                for t in range(TT):
                    nc.vector.tensor_tensor(y[:, t], ps_y[:, t], y[:, t], ALU.add).then_inc(y_evacuated, 1)

            for t in range(TT):
                if t == 0:
                    scale_ctx(0)
                    for c in range(KC):
                        dve.wait_ge(wo_hi_ready, c + 1)
                        nc.vector.tensor_tensor(wo[1][:, c], wo[1][:, c].bitcast(F32), wo[0][:, c].bitcast(F32),
                                                ALU.subtract).then_inc(wo_split, 1)
                else:
                    scale_ctx(t)
                ctx_lo(t)
                if t < 2:
                    split_ffn_lo(t)
                residual(0, t, RING_PRE)
                dve.wait_ge(ln_stats, t + 1)
                mean()
                normalise(t, t)
            for kc in range(KC):
                xt_lo(0, kc, RING_PRE)
            iteration(0, True)
            with dve.Fori(1, B - 1) as b:
                iteration(b, True)
            iteration(B - 1, False)

        @block.tensor
        def _(pe):
            PRODUCTS = ((0, 0), (0, 1), (1, 0))

            def three_products(out, weights, moving, chunks):
                for c in range(chunks):
                    for n, (w, m) in enumerate(PRODUCTS):
                        mm = nc.tensor.matmul(out, weights(w, c), moving(m, c), start=(c == 0 and n == 0),
                                              stop=(c == chunks - 1 and n == 2))
                return mm

            def wait_bank(unit, units, b):
                order = list(units)
                if unit >= BANKS:
                    name, t = order[unit - BANKS]
                    wait_read(name, t, b, units)
                elif units is not RING_PRE:
                    k = unit % BANKS
                    if isinstance(b, int) and b == 0:
                        name, t = list(RING_PRE)[len(RING_PRE) - BANKS + k]
                    else:
                        name, t = [u for u, q in RING_FULL.items() if q % BANKS == k][-1]
                    wait_read(name, t, b - 1, None)

            def wait_read(name, t, b, units):
                ahead = 0 if units is RING_PRE else 1
                if name == "gate":
                    pe.wait_ge(silu_done, FT * b + t + 1)
                elif name == "up":
                    pe.wait_ge(h_ready, FT * b + t + 1)
                elif name == "wo":
                    pe.wait_ge(x1_ready, TT * (b + ahead) + t + 1)
                else:
                    pe.wait_ge(xt_ready, KC * (b + ahead) + t + 1)

            def project_out(b, t, units, at):
                unit = units["wo", t]
                pe.wait_ge(ctx_lo_ready, TT * b + t + 1)
                wait_bank(unit, units, at)
                three_products(bank[unit % BANKS][:], lambda w, c: ctx_t[w][:, c, :], lambda m, c: wo[m][:, c, :],
                               KC).then_inc(wo_done, 1)

            def transposed_x(b, kc, units, at):
                unit = units["T", kc]
                pe.wait_ge(xn_ready, TT * (b + 1))
                wait_bank(unit, units, at)
                for t in range(TT):
                    mm = nc.tensor.transpose(bank[unit % BANKS][:, P * t:P * (t + 1)],
                                             xn[:, t, P * kc:P * (kc + 1)], ident[:])
                mm.then_inc(xt_done, 1)

            def down(b, f):
                n, m, r = FT * b + f, FW[f], f % 2
                pe.wait_ge(h_lo_ready, n + 1)
                if f == 0 and (not isinstance(b, int) or b > 0):
                    pe.wait_ge(y_evacuated, TT * b)
                for t in range(TT):
                    for k, (w, p) in enumerate(PRODUCTS):
                        mm = nc.tensor.matmul(ps_y[:, t], h_parts[w][0:m, r, P * t:P * (t + 1)], wd[p][0:m, f, :],
                                              start=(f == 0 and k == 0), stop=(f == FT - 1 and k == 2))
                mm.then_inc(down_done, 1)

            def iteration(b, has_next):
                units = RING_FULL if has_next else RING_LAST
                first = isinstance(b, int) and b == 0
                pe.wait_ge(xt_ready, KC * (b + 1))
                for f in range(FT):
                    m = FW[f]
                    if first:
                        pe.wait_ge(ffn_split, 3 * (f + 1))
                    for name, w, ready in (("gate", wg, gate_ready), ("up", wu, up_ready)):
                        unit = units[name, f]
                        wait_bank(unit, units, b)
                        three_products(bank[unit % BANKS][0:m, :], lambda q, c: w[q][:, c, P * f:P * f + m],
                                       lambda q, c: xt[q][:, c, :], KC).then_inc(ready, 1)
                    if has_next and 0 <= f - WO_SLOT < TT:
                        project_out(b + 1, f - WO_SLOT, units, b)
                    if f >= 1:
                        down(b, f - 1)
                if has_next:
                    for kc in range(KC):
                        transposed_x(b + 1, kc, units, b)
                down(b, FT - 1)

            pe.wait_ge(ident_ready, 1)
            pe.wait_ge(wo_split, KC)
            for t in range(TT):
                project_out(0, t, RING_PRE, 0)
            for kc in range(KC):
                transposed_x(0, kc, RING_PRE, 0)
            iteration(0, True)
            with pe.Fori(1, B - 1) as b:
                iteration(b, True)
            iteration(B - 1, False)


def build(nc, d):
    phase_1(nc, d)
    phase_2(nc, d)


def rope_tables():
    import numpy as np
    f = np.float32
    theta, factor, lo, hi, length = 500000.0, 32.0, 1.0, 4.0, 1024
    at = np.arange(0, DH, 2, dtype=f) / f(DH)
    freq = f(1.0 / (2.0 * np.pi)) * np.power(f(theta), -at)
    low, high = f(lo / length), f(hi / length)
    scaled = np.where(freq < low, freq / f(factor), freq)
    smooth = np.clip((f(length) * freq - f(lo)) / f(hi - lo), f(0), f(1))
    blended = (f(1) - smooth) * (freq / f(factor)) + smooth * freq
    freq = np.where((freq >= low) & (freq <= high), blended, scaled).astype(f)
    phase = f(2.0 * np.pi) * np.arange(T, dtype=f)[None, :] * freq[:, None]
    cos, sin = np.cos(phase), np.sin(phase)
    heads = P // DH
    return (np.tile(np.concatenate([cos, cos]), (heads, 1)).astype(f),
            np.tile(np.concatenate([-sin, sin]), (heads, 1)).astype(f))


def kernel(L0_attn_resid, L0_attn_Wq, L0_attn_Wk, L0_attn_Wv, L0_attn_Wo, L0_ffn_W_gate, L0_ffn_W_up,
           L0_ffn_W_down):
    import numpy as np
    import concourse.bacc as bacc
    from concourse.bass_utils import run_bass_kernel_spmd

    nc = bacc.Bacc("TRN2", target_bir_lowering=False, num_devices=1)
    cos, sin = rope_tables()
    given = {"x": L0_attn_resid, "wq": L0_attn_Wq, "wk": L0_attn_Wk, "wv": L0_attn_Wv, "wo": L0_attn_Wo,
             "wg": np.asarray(L0_ffn_W_gate).T, "wu": np.asarray(L0_ffn_W_up).T,
             "wd": np.asarray(L0_ffn_W_down).T, "cos": cos, "sin": sin}
    arrays, d = {}, {}
    for name, a in given.items():
        a = np.ascontiguousarray(a)
        arrays[f"in_{name}"] = a
        d[name] = nc.dram_tensor(f"in_{name}", a.shape, F32, kind="ExternalInput").ap()
    for name, shape in (("q_parts", (B, 2, D, T)), ("k_parts", (B, 2, KVW, T)), ("o", (B, D, T)),
                        ("sums", (B, D, T)), ("x1", (B, T, D)), ("wo_raw", (D, D)), ("wg_raw", (D, F)),
                        ("wu_raw", (D, F)), ("wd_raw", (F, D))):
        d[name] = nc.dram_tensor(f"scratch_{name}", shape, F32, kind="Internal").ap()
    d["out"] = nc.dram_tensor("out", (B, T, D), F32, kind="ExternalOutput").ap()
    build(nc, d)
    r = run_bass_kernel_spmd(nc, [arrays], core_ids=[0])
    return r.results[0]["out"]
```

```python
from contextlib import ExitStack

import concourse.bass as bass
from concourse import mybir

F32 = mybir.dt.float32
F32R = mybir.dt.float32r
BF16 = mybir.dt.bfloat16
AXIS = mybir.AxisListType
ALU = mybir.AluOpType
ACT = mybir.ActivationFunctionType

P = 128
B, T, D = 4, 512, 512
NKV, GROUP, DH = 8, 4, 16
F = 1376
TT, KC = T // P, D // P
QT = D // P
KVW = NKV * DH
FT = -(-F // P)
FW = [min(P, F - P * f) for f in range(FT)]
SCALE = float(DH) ** -0.5
EPS = 1e-5
MASKED = -1.0e30
SCORES = TT * GROUP
CHUNK_N = [T - P * c for c in range(TT)]
CHUNK_AT = [sum(CHUNK_N[:c]) for c in range(TT + 1)]
HEADS_MAX = [2 if 2 * n <= T else 1 for n in CHUNK_N]
MAX_AT = [sum(GROUP // h for h in HEADS_MAX[:i]) for i in range(TT + 1)]
MAXIMA = MAX_AT[TT]
ROWS = 3 * DH
PAIR = 2 * ROWS
PAIR_M = PAIR + 2
RING = 4
DMA = 16

STATS_SLOT, MEAN_SLOT, APPLY_SLOT = 1, 5, 6
UNIT_SLOT = {9: ("T", 0), 10: ("T", 1), 11: ("T", 2), 13: ("T", 3), 14: ("R", 0), 17: ("R", 1),
             19: ("R", 2), 22: ("V", 0), 25: ("R", 3), 27: ("R", 4)}
N_ROPE = 1 + QT


def unit_numbers(slots):
    number, n = {}, 0
    for s in range(TT * NKV):
        if s % TT == 0:
            number[s] = n
            n += 1
        elif s in slots:
            number[s] = n
            n += 1
    return number, n


UNIT_NO, UNITS = unit_numbers(UNIT_SLOT)
PRE_UNITS = KC + N_ROPE + 1 + 1


def positive(count):
    return not isinstance(count, int) or count > 0


def phase_1(nc, d):
    with ExitStack() as ctx:
        def sb(name, shape, dt=F32):
            return ctx.enter_context(nc.sbuf_tensor(name, shape, dt))

        def psum(name, shape):
            return ctx.enter_context(nc.psum_tensor(name, shape, F32))

        def sem(name):
            return ctx.enter_context(nc.semaphore(name))

        ident = sb("ident", [P, P])
        ident_b = sb("ident_b", [P, P], BF16)
        mask_q = sb("mask_q", [P, P], BF16)
        mask_k = sb("mask_k", [P, P], BF16)
        half = sb("half", [P, TT])
        eps = sb("eps", [P, TT])
        cos = sb("cos", [P, T])
        sin = sb("sin", [P, T])
        w_raw = sb("w_raw", [P, KC, D + 2 * KVW])
        w_hi = sb("w_hi", [P, KC, D + 2 * KVW], F32R)
        w_lo = sb("w_lo", [P, KC, D + 2 * KVW], F32R)
        x_in = sb("x_in", [P, TT, D])
        stats = sb("stats", [P, TT, 6])
        mean_var = sb("mean_var", [P, TT, 2])
        var_eps = sb("var_eps", [P, TT])
        rstd = sb("rstd", [P, TT])
        xn = sb("xn", [P, TT, D])
        xt_hi = sb("xt_hi", [P, KC, T], F32R)
        xt_lo = sb("xt_lo", [P, KC, T], F32R)
        rot_c = sb("rot_c", [P, 2, T])
        rot_s = sb("rot_s", [P, 2, T])
        r_hi = sb("r_hi", [P, 2, T], F32R)
        r_lo = sb("r_lo", [P, 2, T], F32R)
        v_next = sb("v_next", [P, TT, KVW])
        v_ones = sb("v_ones", [P, TT, NKV, 2 * DH])
        q_rows = [sb(f"q_rows{r}", [PAIR_M, GROUP, T]) for r in range(RING)]
        k_rows = [sb(f"k_rows{r}", [PAIR_M, T]) for r in range(RING)]
        m_raw = sb("m_raw", [P, 2, SCORES])
        m_parts = sb("m_parts", [P, 2, TT, 2, GROUP])
        m_t = [sb(f"m_t{r}", [2 * GROUP, T]) for r in range(2)]
        probs = sb("probs", [P, 2, GROUP, CHUNK_AT[TT]])
        o_sb = sb("o_sb", [P, 2, T])

        ps_s = psum("ps_s", [P, 2, T])
        ps_t = psum("ps_t", [P, GROUP, T])
        ps_o = psum("ps_o", [P, T])
        ps_d = psum("ps_d", [P, T])

        consts_ready = sem("consts_ready")
        const_step = sem("const_step")
        rows_cleared = sem("rows_cleared")
        tables_loaded = sem("tables_loaded")
        w_loaded = sem("w_loaded")
        w_hi_ready = sem("w_hi_ready")
        w_split = sem("w_split")
        raw_copied = sem("raw_copied")
        x_loaded = sem("x_loaded")
        ln_stats = sem("ln_stats")
        ln_mean = sem("ln_mean")
        var_ready = sem("var_ready")
        rstd_ready = sem("rstd_ready")
        xn_ready = sem("xn_ready")
        dense_ready = sem("dense_ready")
        dense_evacuated = sem("dense_evacuated")
        xt_hi_ready = sem("xt_hi_ready")
        rope_sin = sem("rope_sin")
        rope_done = sem("rope_done")
        r_hi_ready = sem("r_hi_ready")
        r_lo_ready = sem("r_lo_ready")
        r_stored = [sem(f"r_stored{k}") for k in range(N_ROPE)]
        v_ready = sem("v_ready")
        rows_staged = [sem(f"rows_staged{r}") for r in range(RING)]
        scores_ready = sem("scores_ready")
        max_done = sem("max_done")
        m_hi_ready = sem("m_hi_ready")
        m_split = sem("m_split")
        m_staged = [sem(f"m_staged{r}") for r in range(2)]
        scores_t_ready = sem("scores_t_ready")
        exp_done = sem("exp_done")
        pv_done = sem("pv_done")
        o_evacuated = sem("o_evacuated")
        o_stored = [sem(f"o_stored{r}") for r in range(2)]

        R_STORE = 3 * DMA
        ROW_DMAS = 4 * DMA

        block = ctx.enter_context(nc.Block())

        @block.sync
        def _(sp):
            sp.dma_start(x_in[:], d["x"][0].rearrange("(t p) n -> p t n", p=P)).then_inc(x_loaded, DMA)
            for at, name, width in ((0, "wq", D), (D, "wk", KVW), (D + KVW, "wv", KVW)):
                sp.dma_start(w_raw[:, :, at:at + width],
                             d[name].rearrange("(c p) n -> p c n", p=P)).then_inc(w_loaded, DMA)
            sp.dma_start(cos[:], d["cos"]).then_inc(tables_loaded, DMA)
            sp.dma_start(sin[:], d["sin"]).then_inc(tables_loaded, DMA)
            def store_rotated(b, k):
                sp.wait_ge(r_lo_ready, N_ROPE * b + k + 1)
                to = d["k_parts"][b] if k == 0 else d["q_parts"][b, P // DH * (k - 1):P // DH * k]
                for part, tile in enumerate((r_hi, r_lo, r_hi) if k == 0 else (r_hi, r_hi, r_lo)):
                    sp.dma_start(to[:, part], tile[:, k % 2, :].bitcast(F32)).then_inc(r_stored[k], DMA)

            def stage_rows(b, g, n):
                used = SCORES * (n - RING + 1)
                if not isinstance(used, int):
                    sp.compute_val(used)
                if g == 0:
                    sp.wait_ge(r_stored[0], R_STORE * (b + 1))
                if g % 2 == 0:
                    sp.wait_ge(r_stored[1 + g // 2], R_STORE * (b + 1))
                if positive(used):
                    sp.wait_ge(scores_t_ready, used)
                r = g % RING
                heads = d["q_parts"][b, GROUP * g:GROUP * (g + 1)].rearrange("(i s) p w t -> s (p w) i t", s=2)
                for s in range(2):
                    sp.dma_start(q_rows[r][ROWS * s:ROWS * (s + 1), s:GROUP:2, :], heads[s]
                                 ).then_inc(rows_staged[r], DMA)
                for s in range(2):
                    sp.dma_start(k_rows[r][ROWS * s:ROWS * (s + 1), :],
                                 d["k_parts"][b, g].rearrange("p w t -> (p w) t")).then_inc(rows_staged[r], DMA)

            def stage_max(g, unit):
                sp.wait_ge(dense_evacuated, unit + 1)
                sp.dma_start(q_rows[g % RING][PAIR:PAIR_M], m_t[g % 2][:]).then_inc(m_staged[g % 2], DMA)

            def store_o(b, g):
                sp.wait_ge(o_evacuated, NKV * b + g + 1)
                sp.dma_start(d["o"][b, g], o_sb[:, g % 2, :]).then_inc(o_stored[g % 2], DMA)

            def iteration(b, has_next):
                if has_next:
                    sp.wait_ge(xn_ready, TT * (b + 1))
                    sp.dma_start(x_in[:], d["x"][b + 1].rearrange("(t p) n -> p t n", p=P)).then_inc(x_loaded, DMA)
                for slot in range(TT * NKV):
                    g, i = slot // TT, slot % TT
                    unit0 = UNITS * b + PRE_UNITS
                    if i == 1 and (has_next or g < NKV - 1):
                        stage_max(g + 1, unit0 + (UNIT_NO[slot - 1] if has_next else g))
                    if i == 1 and g >= 1:
                        store_o(b, g - 1)
                    if has_next and UNIT_SLOT.get(slot - 3, "-")[0] == "R":
                        store_rotated(b + 1, UNIT_SLOT[slot - 3][1])
                    if i == 2 and g + 3 < NKV:
                        stage_rows(b, g + 3, NKV * b + g + 3)
                    if i == 2 and g + 3 >= NKV and has_next:
                        stage_rows(b + 1, g + 3 - NKV, NKV * b + g + 3)
                store_o(b, NKV - 1)

            sp.wait_ge(rows_cleared, RING)
            for k in range(N_ROPE):
                store_rotated(0, k)
                if k in (1, 2):
                    for g in range(2 * (k - 1), min(2 * k, 3)):
                        stage_rows(0, g, g)
            stage_max(0, PRE_UNITS - 1)
            for name in ("wo", "wg", "wu", "wd"):
                sp.dma_start(d[name + "_raw"], d[name]).then_inc(raw_copied, DMA)
            iteration(0, True)
            with sp.Fori(1, B - 1) as b:
                iteration(b, True)
            iteration(B - 1, False)
            for stored in o_stored:
                sp.wait_ge(stored, DMA * NKV // 2 * B)
            sp.wait_ge(raw_copied, 4 * DMA)
            for stored in r_stored:
                sp.wait_ge(stored, R_STORE * B)

        @block.gpsimd
        def _(pool):
            pool.memset(half[:], -0.5)
            pool.memset(eps[:], EPS)
            pool.memset(v_ones[:], 1.0)
            pool.memset(ident[:], 0.0)
            pool.memset(ident_b[:], 0.0)
            pool.memset(mask_q[:], 0.0)
            pool.memset(mask_k[:], 0.0).then_inc(const_step, 1)
            pool.wait_ge(const_step, 1)
            for tile in (ident, ident_b):
                nc.gpsimd.affine_select(out=tile[:], in_=tile[:], compare_op=ALU.not_equal, fill=1.0, base=0,
                                        pattern=[[-1, P]], channel_multiplier=1)
            nc.gpsimd.affine_select(out=mask_q[:], in_=mask_q[:], compare_op=ALU.is_ge, fill=MASKED, base=0,
                                    pattern=[[-1, P]], channel_multiplier=1)
            nc.gpsimd.affine_select(out=mask_k[:], in_=mask_k[:], compare_op=ALU.is_ge, fill=MASKED, base=0,
                                    pattern=[[1, P]], channel_multiplier=-1).then_inc(consts_ready, 1)
            pool.wait_ge(consts_ready, 1)

            def layernorm_scale(b):
                pool.wait_ge(ln_mean, TT * (b + 1))
                nc.gpsimd.tensor_tensor(var_eps[:], mean_var[:, :, 1], eps[:], ALU.add).then_inc(var_ready, 1)
                pool.wait_ge(var_ready, b + 1)
                nc.gpsimd.tensor_tensor(rstd[:], var_eps[:], half[:], ALU.pow).then_inc(rstd_ready, 1)

            def rotate(b, k, unit):
                r = k % 2
                pool.wait_ge(dense_evacuated, unit + 1)
                nc.gpsimd.tensor_tensor(rot_s[:, r], rot_s[:, r], sin[:], ALU.mult).then_inc(rope_sin, 1)
                pool.wait_ge(rope_sin, N_ROPE * b + k + 1)
                nc.gpsimd.tensor_tensor(rot_c[:, r], rot_c[:, r], rot_s[:, r], ALU.add).then_inc(rope_done, 1)

            pool.wait_ge(tables_loaded, 2 * DMA)
            layernorm_scale(0)
            for k in range(N_ROPE):
                rotate(0, k, KC + k)
            with pool.Fori(0, B - 1) as b:
                layernorm_scale(b + 1)
                for slot, (kind, k) in UNIT_SLOT.items():
                    if kind == "R":
                        rotate(b + 1, k, UNITS * b + PRE_UNITS + UNIT_NO[slot])

        @block.scalar
        def _(act):
            def xt_high(unit, kc):
                act.wait_ge(dense_ready, unit + 1)
                nc.scalar.copy(xt_hi[:, kc], ps_d[:]).then_inc(xt_hi_ready, 1)

            def rotated_high(b, k):
                act.wait_ge(rope_done, N_ROPE * b + k + 1)
                if k >= 2:
                    act.wait_ge(r_stored[k - 2], R_STORE * (b + 1))
                elif not isinstance(b, int):
                    act.wait_ge(r_stored[N_ROPE - 1 - k], R_STORE * b)
                nc.scalar.copy(r_hi[:, k % 2], rot_c[:, k % 2]).then_inc(r_hi_ready, 1)

            def v_evacuate(unit):
                act.wait_ge(dense_ready, unit + 1)
                nc.scalar.copy(v_next[:].rearrange("p t n -> p (t n)"), ps_d[:]).then_inc(dense_evacuated, 1)

            def v_place(b, unit):
                act.wait_ge(dense_evacuated, unit + 1)
                nc.scalar.copy(v_ones[:, :, :, 0:DH].rearrange("p t h w -> p (t h) w"),
                               v_next[:].rearrange("p t (h w) -> p (t h) w", w=DH)).then_inc(v_ready, 1)

            def max_evacuate(b, g, unit):
                act.wait_ge(dense_ready, unit + 1)
                if not isinstance(b, int) or b >= 1 or g >= 2:
                    act.wait_ge(m_staged[g % 2], DMA * (NKV // 2 * b + g // 2))
                nc.scalar.copy(m_t[g % 2][:], ps_d[0:2 * GROUP, :]).then_inc(dense_evacuated, 1)

            def exponentials(b, g, c):
                for j in range(GROUP):
                    n = SCORES * (NKV * b + g) + GROUP * c + j
                    if c == 0 and j == 0:
                        if positive(NKV * b + max(g - 1, 0)):
                            act.wait_ge(pv_done, NKV * b + max(g - 1, 0))
                    act.wait_ge(scores_t_ready, n + 1)
                    nc.scalar.activation(probs[:, g % 2, j, CHUNK_AT[c]:CHUNK_AT[c + 1]],
                                         ps_t[:, j, 0:CHUNK_N[c]], ACT.Exp, scale=SCALE).then_inc(exp_done, 1)

            def o_evacuate(b, g):
                act.wait_ge(pv_done, NKV * b + g + 1)
                if positive(NKV // 2 * b + g // 2):
                    act.wait_ge(o_stored[g % 2], DMA * (NKV // 2 * b + g // 2))
                nc.scalar.copy(o_sb[:, g % 2], ps_o[:]).then_inc(o_evacuated, 1)

            def iteration(b, has_next):
                unit0 = UNITS * b + PRE_UNITS
                for slot in range(TT * NKV):
                    g, i = slot // TT, slot % TT
                    if i == 1 and (has_next or g < NKV - 1):
                        max_evacuate(b, g + 1, unit0 + (UNIT_NO[slot - 1] if has_next else g))
                    kind, k = UNIT_SLOT.get(slot - 1, "--")
                    if has_next and kind == "T":
                        xt_high(unit0 + UNIT_NO[slot - 1], k)
                    if has_next and kind == "V":
                        v_evacuate(unit0 + UNIT_NO[slot - 1])
                    if i == 1 and g >= 1:
                        o_evacuate(b, g - 1)
                    exponentials(b, g, i)
                    kind, k = UNIT_SLOT.get(slot - 2, "--")
                    if has_next and kind == "R":
                        rotated_high(b + 1, k)
                o_evacuate(b, NKV - 1)
                if has_next:
                    v_place(b, unit0 + UNIT_NO[[s for s, u in UNIT_SLOT.items() if u[0] == "V"][0]])

            act.wait_ge(w_loaded, 3 * DMA)
            for c in range(KC):
                nc.scalar.copy(w_hi[:, c], w_raw[:, c]).then_inc(w_hi_ready, 1)
            for kc in range(KC):
                xt_high(kc, kc)
            for k in range(N_ROPE):
                rotated_high(0, k)
            v_evacuate(KC + N_ROPE)
            act.wait_ge(consts_ready, 1)
            v_place(0, KC + N_ROPE)
            max_evacuate(0, 0, PRE_UNITS - 1)
            iteration(0, True)
            with act.Fori(1, B - 1) as b:
                iteration(b, True)
            iteration(B - 1, False)

        @block.vector
        def _(dve):
            swap = [(p + DH // 2) % DH + DH * (p // DH) for p in range(32)]

            def layernorm_stats(b, t):
                dve.wait_ge(x_loaded, DMA * (b + 1))
                nc.vector.bn_stats(stats[:, t], x_in[:, t]).then_inc(ln_stats, 1)

            def layernorm_mean():
                for t in range(TT):
                    nc.vector.bn_aggr(mean_var[:, t], stats[:, t]).then_inc(ln_mean, 1)

            def layernorm_apply(b, t):
                dve.wait_ge(rstd_ready, b + 1)
                nc.vector.tensor_scalar(xn[:, t], x_in[:, t], mean_var[:, t, 0:1], rstd[:, t:t + 1],
                                        ALU.subtract, ALU.mult).then_inc(xn_ready, 1)

            def xt_low(b, kc):
                dve.wait_ge(xt_hi_ready, KC * b + kc + 1)
                nc.vector.tensor_tensor(xt_lo[:, kc], ps_d[:], xt_hi[:, kc].bitcast(F32),
                                        ALU.subtract).then_inc(dense_evacuated, 1)

            def rope_parts(b, k, unit):
                r = k % 2
                if k >= 2:
                    dve.wait_ge(r_lo_ready, N_ROPE * b + k - 1)
                elif not isinstance(b, int):
                    dve.wait_ge(r_lo_ready, N_ROPE * b)
                dve.wait_ge(dense_ready, unit + 1)
                nc.vector.tensor_tensor(rot_c[:, r], ps_d[:], cos[:], ALU.mult)
                nc.vector.stream_shuffle(rot_s[:, r], ps_d[:], swap).then_inc(dense_evacuated, 1)

            def rotated_low(b, k):
                r = k % 2
                dve.wait_ge(r_hi_ready, N_ROPE * b + k + 1)
                nc.vector.tensor_tensor(r_lo[:, r], rot_c[:, r], r_hi[:, r].bitcast(F32),
                                        ALU.subtract).then_inc(r_lo_ready, 1)

            def row_max(n, g, i):
                heads, width = HEADS_MAX[i], CHUNK_N[i]
                for u in range(GROUP // heads):
                    at = GROUP * (TT - 1 - i) + heads * u
                    dve.wait_ge(scores_ready, MAXIMA * n + MAX_AT[i] + u + 1)
                    nc.vector.tensor_reduce(
                        out=m_raw[:, g % 2, at:at + heads], op=ALU.max, axis=AXIS.X,
                        in_=ps_s[:, u % 2, 0:heads * width].rearrange("p (j t) -> p j t", j=heads)
                    ).then_inc(max_done, 1)

            def split_max(n, g):
                r = g % 2
                raw = m_raw[:, r, :].rearrange("p (q j) -> p q j", j=GROUP)
                hi = m_parts[:, r, :, 0, :]
                lo = m_parts[:, r, :, 1, :]
                dve.wait_ge(max_done, MAXIMA * (n + 1))
                nc.vector.tensor_copy(hi.bitcast(F32R), raw).then_inc(m_hi_ready, 1)
                dve.wait_ge(m_hi_ready, n + 1)
                nc.vector.tensor_tensor(lo.bitcast(F32R), raw, hi, ALU.subtract).then_inc(m_split, 1)

            def iteration(b, has_next):
                unit0 = UNITS * b + PRE_UNITS
                for slot in range(TT * NKV):
                    g, i = slot // TT, slot % TT
                    kind, k = UNIT_SLOT.get(slot - 3, "--")
                    if has_next and kind == "R":
                        rotated_low(b + 1, k)
                    kind, k = UNIT_SLOT.get(slot - 1, "--")
                    if has_next and kind == "T":
                        xt_low(b + 1, k)
                    if has_next and kind == "R":
                        rope_parts(b + 1, k, unit0 + UNIT_NO[slot - 1])
                    if has_next and slot == MEAN_SLOT:
                        dve.wait_ge(ln_stats, TT * (b + 2))
                    if has_next or g < NKV - 2:
                        row_max(NKV * b + g + 2, g, i)
                        if i == TT - 1:
                            split_max(NKV * b + g + 2, g)
                    if has_next and 0 <= slot - STATS_SLOT < TT:
                        layernorm_stats(b + 1, slot - STATS_SLOT)
                    if has_next and slot == MEAN_SLOT:
                        layernorm_mean()
                    if has_next and 0 <= slot - APPLY_SLOT < TT // 2:
                        for t in range(2):
                            layernorm_apply(b + 1, 2 * (slot - APPLY_SLOT) + t)

            for r in range(RING):
                nc.vector.memset(q_rows[r][0:PAIR], 0.0)
                nc.vector.memset(k_rows[r][PAIR:PAIR_M], -1.0).then_inc(rows_cleared, 1)
            for t in range(TT):
                layernorm_stats(0, t)
            dve.wait_ge(ln_stats, TT)
            layernorm_mean()
            for t in range(TT):
                layernorm_apply(0, t)
            for c in range(KC):
                dve.wait_ge(w_hi_ready, c + 1)
                nc.vector.tensor_tensor(w_lo[:, c], w_raw[:, c], w_hi[:, c].bitcast(F32),
                                        ALU.subtract).then_inc(w_split, 1)
            for kc in range(KC):
                xt_low(0, kc)
            dve.wait_ge(tables_loaded, 2 * DMA)
            for k in range(N_ROPE):
                if k >= 2:
                    rotated_low(0, k - 2)
                rope_parts(0, k, KC + k)
            rotated_low(0, N_ROPE - 2)
            rotated_low(0, N_ROPE - 1)
            dve.wait_ge(consts_ready, 1)
            for g in range(2):
                for i in range(TT):
                    row_max(g, g, i)
                split_max(g, g)
            iteration(0, True)
            with dve.Fori(1, B - 1) as b:
                iteration(b, True)
            iteration(B - 1, False)

        @block.tensor
        def _(pe):
            PRODUCTS = ((0, 0), (0, 1), (1, 0))
            W, X = (w_hi, w_lo), (xt_hi, xt_lo)

            def bank_free(unit, piece):
                if piece == 0 and positive(unit):
                    pe.wait_ge(dense_evacuated, unit)

            def transposed_x(b, kc, unit, t):
                if t == 0:
                    pe.wait_ge(xn_ready, TT * (b + 1))
                bank_free(unit, t)
                mm = nc.tensor.transpose(ps_d[:, P * t:P * (t + 1)], xn[:, t, P * kc:P * (kc + 1)], ident[:])
                if t == TT - 1:
                    mm.then_inc(dense_ready, 1)

            def project(k, unit, c):
                at = D if k == 0 else P * (k - 1)
                bank_free(unit, c)
                for n, (w, x) in enumerate(PRODUCTS):
                    mm = nc.tensor.matmul(ps_d[:], W[w][:, c, at:at + P], X[x][:, c, :], start=(c == 0 and n == 0),
                                          stop=(c == KC - 1 and n == 2))
                if c == KC - 1:
                    mm.then_inc(dense_ready, 1)

            def project_v(unit, t):
                bank_free(unit, t)
                for c in range(KC):
                    for n, (w, x) in enumerate(PRODUCTS):
                        mm = nc.tensor.matmul(ps_d[:, KVW * t:KVW * (t + 1)], X[x][:, c, P * t:P * (t + 1)],
                                              W[w][:, c, D + KVW:D + 2 * KVW], start=(c == 0 and n == 0),
                                              stop=(c == KC - 1 and n == 2))
                if t == TT - 1:
                    mm.then_inc(dense_ready, 1)

            def dense(b, kind, k, unit, piece):
                if kind == "T":
                    transposed_x(b, k, unit, piece)
                elif kind == "R":
                    project(k, unit, piece)
                else:
                    project_v(unit, piece)

            def scores(b, g, i, j):
                n = NKV * b + g
                r, q = g % RING, TT - 1 - i
                heads, width = HEADS_MAX[i], CHUNK_N[i]
                u, place = j // heads, j % heads
                if i == 0 and j == 0:
                    pe.wait_ge(rows_staged[r], ROW_DMAS * (NKV // RING * b + g // RING + 1))
                before = MAXIMA * n + MAX_AT[i] + u - 1
                if place == 0 and positive(before):
                    pe.wait_ge(max_done, before)
                out = ps_s[:, u % 2, width * place:width * (place + 1)]
                nc.tensor.matmul(out, q_rows[r][0:PAIR, j, P * q:P * (q + 1)].bitcast(F32R),
                                 k_rows[r][0:PAIR, 0:width].bitcast(F32R), start=True, stop=False)
                mm = nc.tensor.matmul(out[:, P * q:width], ident_b[:], mask_q[:], start=False, stop=True)
                if place == heads - 1:
                    mm.then_inc(scores_ready, 1)

            def transposed_max(n, g, unit):
                pe.wait_ge(m_split, n + 1)
                bank_free(unit, 0)
                for q in range(TT):
                    mm = nc.tensor.transpose(ps_d[0:2 * GROUP, P * q:P * (q + 1)],
                                             m_parts[:, g % 2, q].rearrange("p w j -> p (w j)"), ident[:])
                mm.then_inc(dense_ready, 1)

            def scores_t(b, g, c, j):
                n = NKV * b + g
                r = g % RING
                if c == 0 and j == 0:
                    pe.wait_ge(m_staged[g % 2], DMA * (NKV // 2 * b + g // 2 + 1))
                if g == 0 and c == 0:
                    if positive(n):
                        pe.wait_ge(exp_done, SCORES * n)
                else:
                    pe.wait_ge(exp_done, SCORES * n + GROUP * c + j - GROUP + 1)
                out = ps_t[:, j, 0:CHUNK_N[c]]
                nc.tensor.matmul(out, k_rows[r][:, P * c:P * (c + 1)].bitcast(F32R),
                                 q_rows[r][:, j, P * c:T].bitcast(F32R), start=True, stop=False)
                nc.tensor.matmul(ps_t[:, j, 0:P], ident_b[:], mask_k[:], start=False,
                                 stop=True).then_inc(scores_t_ready, 1)

            def weighted_v(b, g, c):
                n = NKV * b + g
                pe.wait_ge(exp_done, SCORES * n + GROUP * (c + 1))
                if c == 0:
                    if positive(n):
                        pe.wait_ge(o_evacuated, n)
                    if g == 0:
                        pe.wait_ge(v_ready, b + 1)
                for j in range(GROUP):
                    mm = nc.tensor.matmul(ps_o[32 * j:32 * j + 2 * DH, P * c:T], v_ones[:, c, g, :],
                                          probs[:, g % 2, j, CHUNK_AT[c]:CHUNK_AT[c + 1]],
                                          start=(c == 0), stop=(c == TT - 1))
                if c == TT - 1:
                    mm.then_inc(pv_done, 1)

            def iteration(b, has_next):
                unit0 = UNITS * b + PRE_UNITS
                for slot in range(TT * NKV):
                    g, i = slot // TT, slot % TT
                    kind, k = UNIT_SLOT.get(slot, "--") if has_next else "--"
                    for j in range(GROUP):
                        if has_next or g < NKV - 2:
                            scores(b, g + 2, i, j)
                        scores_t(b, g, i, j)
                        if j == 1 and i >= 1:
                            weighted_v(b, g, i - 1)
                        elif j == 1 and g >= 1:
                            weighted_v(b, g - 1, TT - 1)
                        if kind != "-":
                            dense(b + 1, kind, k, unit0 + UNIT_NO[slot], j)
                    if i == 0 and (has_next or g < NKV - 1):
                        transposed_max(NKV * b + g + 1, g + 1, unit0 + (UNIT_NO[slot] if has_next else g))
                weighted_v(b, NKV - 1, TT - 1)

            pe.wait_ge(consts_ready, 1)
            for unit in range(KC + N_ROPE + 1):
                kind = "T" if unit < KC else "R" if unit < KC + N_ROPE else "V"
                if unit == KC:
                    pe.wait_ge(w_split, KC)
                for piece in range(4):
                    dense(0, kind, unit - KC if kind == "R" else unit, unit, piece)
            for g in range(2):
                for i in range(TT):
                    for j in range(GROUP):
                        scores(0, g, i, j)
            transposed_max(0, 0, PRE_UNITS - 1)
            iteration(0, True)
            with pe.Fori(1, B - 1) as b:
                iteration(b, True)
            iteration(B - 1, False)


WO_SLOT = 3


def ring_units(has_next):
    units = []
    for f in range(FT):
        units += [("gate", f), ("up", f)]
        if has_next and 0 <= f - WO_SLOT < TT:
            units.append(("wo", f - WO_SLOT))
    if has_next:
        units += [("T", kc) for kc in range(KC)]
    return {u: n for n, u in enumerate(units)}


BANKS = 4
RING_PRE = {u: n for n, u in enumerate([("wo", t) for t in range(TT)] + [("T", c) for c in range(KC)])}
RING_FULL = ring_units(True)
RING_LAST = ring_units(False)
assert len(RING_PRE) % BANKS == 0


def phase_2(nc, d):
    with ExitStack() as ctx:
        def sb(name, shape, dt=F32):
            return ctx.enter_context(nc.sbuf_tensor(name, shape, dt))

        def sem(name):
            return ctx.enter_context(nc.semaphore(name))

        wo = [sb(f"wo_{p}", [P, KC, D], F32R) for p in ("hi", "lo")]
        wg = [sb(f"wg_{p}", [P, KC, F], F32R) for p in ("hi", "lo")]
        wu = [sb(f"wu_{p}", [P, KC, F], F32R) for p in ("hi", "lo")]
        wd = [sb(f"wd_{p}", [P, FT, D], F32R) for p in ("hi", "lo")]
        ident = sb("ident2", [P, P])
        half = sb("half2", [P, 1])
        eps = sb("eps2", [P, 1])
        o_in = sb("o_in", [P, QT, P])
        sums = sb("sums_in", [P, QT, P])
        ctx_t = [sb(f"ctx_{p}", [P, QT, P], F32R) for p in ("hi", "lo")]
        x_res = sb("x_res", [P, 2, D])
        xn = sb("xn2", [P, TT, D])
        y = sb("y", [P, TT, D])
        stats = sb("stats2", [P, 6])
        mean_var = sb("mean_var2", [P, 2])
        var_eps = sb("var_eps2", [P, 1])
        rstd = sb("rstd2", [P, 1])
        xt = [sb(f"x2t_{p}", [P, KC, T], F32R) for p in ("hi", "lo")]
        h = sb("h", [P, 2, T])
        h_parts = [sb(f"h_{p}", [P, 2, T], F32R) for p in ("hi", "lo")]
        bank = [ctx.enter_context(nc.psum_tensor(f"bank{k}", [P, T], F32)) for k in range(BANKS)]
        ps_y = ctx.enter_context(nc.psum_tensor("ps_y", [P, TT, D], F32))

        ident_step = sem("ident_step")
        ident_ready = sem("ident_ready")
        wo_loaded = sem("wo_loaded")
        wo_hi_ready = sem("wo_hi_ready")
        wo_split = sem("wo_split")
        ffn_loaded = [sem(f"ffn_loaded{f}") for f in range(FT)]
        ffn_hi_ready = sem("ffn_hi_ready")
        ffn_split = sem("ffn_split")
        o_loaded = sem("o_loaded")
        xres_loaded = [sem(f"xres_loaded{r}") for r in range(2)]
        recip_done = sem("recip_done")
        ctx_scaled = sem("ctx_scaled")
        ctx_hi_ready = sem("ctx_hi_ready")
        ctx_lo_ready = sem("ctx_lo_ready")
        wo_done = sem("wo_done")
        x1_ready = sem("x1_ready")
        x1_stored = sem("x1_stored")
        ln_stats = sem("ln2_stats")
        ln_mean = sem("ln2_mean")
        var_ready = sem("var2_ready")
        rstd_ready = sem("rstd2_ready")
        xn_ready = sem("xn2_ready")
        xt_done = sem("x2t_done")
        xt_hi_ready = sem("x2t_hi_ready")
        xt_ready = sem("x2t_ready")
        gate_ready = sem("gate_ready")
        up_ready = sem("up_ready")
        silu_done = sem("silu_done")
        h_ready = sem("h_ready")
        h_hi_ready = sem("h_hi_ready")
        h_lo_ready = sem("h_lo_ready")
        down_done = sem("down_done")
        y_loaded = sem("y_loaded")
        y_evacuated = sem("y_evacuated")
        y_stored = sem("y_stored")

        W_DMAS = 3 * DMA

        block = ctx.enter_context(nc.Block())

        @block.sync
        def _(sp):
            def load_o(b, t):
                n = TT * b + t
                if not isinstance(n, int) or n >= 1:
                    sp.wait_ge(ctx_lo_ready, n)
                halves = d["o"][b].rearrange("g (j s w) t -> s (g j) w t", j=GROUP, s=2)
                for tile, from_ in ((o_in, halves[0]), (sums, halves[1])):
                    for c in range(KC):
                        sp.dma_start(tile[:, c], from_[P // DH * c:P // DH * (c + 1), :, P * t:P * (t + 1)]
                                     ).then_inc(o_loaded, DMA)

            def load_residual(b, t):
                n = TT * b + t
                if not isinstance(n, int) or n >= 2:
                    sp.wait_ge(x1_ready, n - 1)
                sp.dma_start(x_res[:, t % 2], d["x"][b, P * t:P * (t + 1)]).then_inc(xres_loaded[t % 2], DMA)

            def store_x1(b, t):
                sp.wait_ge(x1_ready, TT * b + t + 1)
                sp.dma_start(d["x1"][b, P * t:P * (t + 1)], xn[:, t]).then_inc(x1_stored, DMA)

            def iteration(b, has_next):
                if not isinstance(b, int) or b > 0:
                    sp.wait_ge(y_stored, TT * DMA * b)
                sp.wait_ge(x1_stored, TT * DMA * (b + 1))
                sp.dma_start(y[:], d["x1"][b].rearrange("(t p) n -> p t n", p=P)).then_inc(y_loaded, DMA)
                if has_next:
                    for t in range(2):
                        load_o(b + 1, t)
                        load_residual(b + 1, t)
                    for t in range(TT):
                        if t + 2 < TT:
                            load_o(b + 1, t + 2)
                        store_x1(b + 1, t)
                        if t + 2 < TT:
                            load_residual(b + 1, t + 2)
                for t in range(TT):
                    sp.wait_ge(y_evacuated, TT * b + t + 1)
                    sp.dma_start(d["out"][b, P * t:P * (t + 1)], y[:, t]).then_inc(y_stored, DMA)

            load_o(0, 0)
            load_residual(0, 0)
            sp.dma_start(wo[1][:].bitcast(F32), d["wo_raw"].rearrange("(c p) n -> p c n", p=P)
                         ).then_inc(wo_loaded, DMA)
            for f in range(FT):
                m = FW[f]
                for w, name in ((wg, "wg_raw"), (wu, "wu_raw")):
                    sp.dma_start(w[1][:, :, P * f:P * f + m].bitcast(F32),
                                 d[name].rearrange("(c p) n -> p c n", p=P)[:, :, P * f:P * f + m]
                                 ).then_inc(ffn_loaded[f], DMA)
                sp.dma_start(wd[1][0:m, f].bitcast(F32), d["wd_raw"][P * f:P * f + m]).then_inc(ffn_loaded[f], DMA)
                if f < TT:
                    if f + 1 < TT:
                        load_o(0, f + 1)
                        load_residual(0, f + 1)
                    store_x1(0, f)
            iteration(0, True)
            with sp.Fori(1, B - 1) as b:
                iteration(b, True)
            iteration(B - 1, False)
            sp.wait_ge(y_stored, TT * DMA * B)
            sp.wait_ge(x1_stored, TT * DMA * B)

        @block.gpsimd
        def _(pool):
            pool.memset(half[:], -0.5)
            pool.memset(eps[:], EPS)
            pool.memset(ident[:], 0.0).then_inc(ident_step, 1)
            pool.wait_ge(ident_step, 1)
            nc.gpsimd.affine_select(out=ident[:], in_=ident[:], compare_op=ALU.not_equal, fill=1.0, base=0,
                                    pattern=[[-1, P]], channel_multiplier=1).then_inc(ident_ready, 1)
            pool.wait_ge(ident_ready, 1)
            with pool.Fori(0, B * TT) as n:
                pool.wait_ge(ln_mean, n + 1)
                nc.gpsimd.tensor_tensor(var_eps[:], mean_var[:, 1:2], eps[:], ALU.add).then_inc(var_ready, 1)
                pool.wait_ge(var_ready, n + 1)
                nc.gpsimd.tensor_tensor(rstd[:], var_eps[:], half[:], ALU.pow).then_inc(rstd_ready, 1)

        @block.scalar
        def _(act):
            def split_ffn_hi(f):
                act.wait_ge(ffn_loaded[f], W_DMAS)
                m = FW[f]
                for w in (wg, wu):
                    nc.scalar.copy(w[0][:, :, P * f:P * f + m], w[1][:, :, P * f:P * f + m].bitcast(F32)
                                   ).then_inc(ffn_hi_ready, 1)
                nc.scalar.copy(wd[0][0:m, f], wd[1][0:m, f].bitcast(F32)).then_inc(ffn_hi_ready, 1)

            def ctx_hi(n):
                act.wait_ge(ctx_scaled, n + 1)
                if not isinstance(n, int) or n >= 1:
                    act.wait_ge(wo_done, n)
                nc.scalar.copy(ctx_t[0][:], o_in[:]).then_inc(ctx_hi_ready, 1)

            def xt_hi(b, kc, units):
                act.wait_ge(xt_done, KC * b + kc + 1)
                nc.scalar.copy(xt[0][:, kc], bank[units["T", kc] % BANKS][:]).then_inc(xt_hi_ready, 1)

            def iteration(b, has_next):
                units = RING_FULL if has_next else RING_LAST
                first = isinstance(b, int) and b == 0
                for f in range(FT):
                    n, m, r = FT * b + f, FW[f], f % 2
                    act.wait_ge(gate_ready, n + 1)
                    if not first or f >= 2:
                        act.wait_ge(h_lo_ready, FT * b if f < 2 else n - 1)
                    nc.scalar.activation(h[0:m, r], bank[units["gate", f] % BANKS][0:m, :], ACT.Silu
                                         ).then_inc(silu_done, 1)
                    act.wait_ge(h_ready, n + 1)
                    if not first or f >= 2:
                        act.wait_ge(down_done, FT * b if f < 2 else n - 1)
                    nc.scalar.copy(h_parts[0][0:m, r], h[0:m, r]).then_inc(h_hi_ready, 1)
                    if first and f + 2 < FT:
                        split_ffn_hi(f + 2)
                    if has_next and 0 <= f - WO_SLOT + 1 < TT:
                        ctx_hi(TT * (b + 1) + f - WO_SLOT + 1)
                if has_next:
                    for kc in range(KC):
                        xt_hi(b + 1, kc, units)

            act.wait_ge(wo_loaded, DMA)
            for c in range(KC):
                nc.scalar.copy(wo[0][:, c], wo[1][:, c].bitcast(F32)).then_inc(wo_hi_ready, 1)
            ctx_hi(0)
            split_ffn_hi(0)
            ctx_hi(1)
            split_ffn_hi(1)
            ctx_hi(2)
            ctx_hi(3)
            for kc in range(KC):
                xt_hi(0, kc, RING_PRE)
            iteration(0, True)
            with act.Fori(1, B - 1) as b:
                iteration(b, True)
            iteration(B - 1, False)

        @block.vector
        def _(dve):
            def split_ffn_lo(f):
                m = FW[f]
                for k, w in enumerate((wg, wu)):
                    at = P * f
                    dve.wait_ge(ffn_hi_ready, 3 * f + k + 1)
                    nc.vector.tensor_tensor(w[1][:, :, at:at + m], w[1][:, :, at:at + m].bitcast(F32),
                                            w[0][:, :, at:at + m].bitcast(F32), ALU.subtract).then_inc(ffn_split, 1)
                dve.wait_ge(ffn_hi_ready, 3 * f + 3)
                nc.vector.tensor_tensor(wd[1][0:m, f], wd[1][0:m, f].bitcast(F32), wd[0][0:m, f].bitcast(F32),
                                        ALU.subtract).then_inc(ffn_split, 1)

            def scale_ctx(n):
                dve.wait_ge(o_loaded, 2 * KC * DMA * (n + 1))
                nc.vector.reciprocal(sums[:], sums[:]).then_inc(recip_done, 1)
                dve.wait_ge(recip_done, n + 1)
                nc.vector.tensor_tensor(o_in[:], o_in[:], sums[:], ALU.mult).then_inc(ctx_scaled, 1)

            def ctx_lo(n):
                dve.wait_ge(ctx_hi_ready, n + 1)
                nc.vector.tensor_tensor(ctx_t[1][:], o_in[:], ctx_t[0][:].bitcast(F32),
                                        ALU.subtract).then_inc(ctx_lo_ready, 1)

            def residual(b, t, units):
                n = TT * b + t
                dve.wait_ge(wo_done, n + 1)
                dve.wait_ge(xres_loaded[t % 2], DMA * (TT // 2 * b + t // 2 + 1))
                k = units["wo", t] % BANKS
                nc.vector.tensor_tensor(xn[:, t], bank[k][:], x_res[:, t % 2], ALU.add
                                        ).then_inc(x1_ready, 1)
                dve.wait_ge(x1_ready, n + 1)
                nc.vector.bn_stats(stats[:], xn[:, t]).then_inc(ln_stats, 1)

            def mean():
                nc.vector.bn_aggr(mean_var[:], stats[:]).then_inc(ln_mean, 1)

            def normalise(n, t):
                dve.wait_ge(rstd_ready, n + 1)
                dve.wait_ge(x1_stored, DMA * (n + 1))
                nc.vector.tensor_scalar(xn[:, t], xn[:, t], mean_var[:, 0:1], rstd[:, 0:1], ALU.subtract,
                                        ALU.mult).then_inc(xn_ready, 1)

            def xt_lo(b, kc, units):
                k = units["T", kc] % BANKS
                dve.wait_ge(xt_hi_ready, KC * b + kc + 1)
                nc.vector.tensor_tensor(xt[1][:, kc], bank[k][:], xt[0][:, kc].bitcast(F32),
                                        ALU.subtract).then_inc(xt_ready, 1)

            def iteration(b, has_next):
                units = RING_FULL if has_next else RING_LAST
                first = isinstance(b, int) and b == 0
                for f in range(FT):
                    n, m, r = FT * b + f, FW[f], f % 2
                    stats_of = f - WO_SLOT - 2
                    normalised = has_next and 0 <= stats_of < TT
                    if normalised:
                        dve.wait_ge(ln_stats, TT * (b + 1) + stats_of + 1)
                    dve.wait_ge(silu_done, n + 1)
                    dve.wait_ge(up_ready, n + 1)
                    nc.vector.tensor_tensor(h[0:m, r], h[0:m, r], bank[units["up", f] % BANKS][0:m, :],
                                            ALU.mult).then_inc(h_ready, 1)
                    if normalised:
                        mean()
                    dve.wait_ge(h_hi_ready, n + 1)
                    nc.vector.tensor_tensor(h_parts[1][0:m, r], h[0:m, r], h_parts[0][0:m, r].bitcast(F32),
                                            ALU.subtract).then_inc(h_lo_ready, 1)
                    if first and f + 2 < FT:
                        split_ffn_lo(f + 2)
                    if has_next:
                        t = f - WO_SLOT + 1
                        if 0 <= t < TT:
                            scale_ctx(TT * (b + 1) + t)
                            ctx_lo(TT * (b + 1) + t)
                        if normalised:
                            normalise(TT * (b + 1) + stats_of, stats_of)
                        if 0 <= t - 2 < TT:
                            residual(b + 1, t - 2, units)
                if has_next:
                    for kc in range(KC):
                        xt_lo(b + 1, kc, units)
                dve.wait_ge(y_loaded, DMA * (b + 1))
                dve.wait_ge(down_done, FT * (b + 1))
                for t in range(TT):
                    nc.vector.tensor_tensor(y[:, t], ps_y[:, t], y[:, t], ALU.add).then_inc(y_evacuated, 1)

            for t in range(TT):
                if t == 0:
                    scale_ctx(0)
                    for c in range(KC):
                        dve.wait_ge(wo_hi_ready, c + 1)
                        nc.vector.tensor_tensor(wo[1][:, c], wo[1][:, c].bitcast(F32), wo[0][:, c].bitcast(F32),
                                                ALU.subtract).then_inc(wo_split, 1)
                else:
                    scale_ctx(t)
                ctx_lo(t)
                if t < 2:
                    split_ffn_lo(t)
                residual(0, t, RING_PRE)
                dve.wait_ge(ln_stats, t + 1)
                mean()
                normalise(t, t)
            for kc in range(KC):
                xt_lo(0, kc, RING_PRE)
            iteration(0, True)
            with dve.Fori(1, B - 1) as b:
                iteration(b, True)
            iteration(B - 1, False)

        @block.tensor
        def _(pe):
            PRODUCTS = ((0, 0), (0, 1), (1, 0))

            def three_products(out, weights, moving, chunks):
                for c in range(chunks):
                    for n, (w, m) in enumerate(PRODUCTS):
                        mm = nc.tensor.matmul(out, weights(w, c), moving(m, c), start=(c == 0 and n == 0),
                                              stop=(c == chunks - 1 and n == 2))
                return mm

            def wait_bank(unit, units, b):
                order = list(units)
                if unit >= BANKS:
                    name, t = order[unit - BANKS]
                    wait_read(name, t, b, units)
                elif units is not RING_PRE:
                    k = unit % BANKS
                    if isinstance(b, int) and b == 0:
                        name, t = list(RING_PRE)[len(RING_PRE) - BANKS + k]
                    else:
                        name, t = [u for u, q in RING_FULL.items() if q % BANKS == k][-1]
                    wait_read(name, t, b - 1, None)

            def wait_read(name, t, b, units):
                ahead = 0 if units is RING_PRE else 1
                if name == "gate":
                    pe.wait_ge(silu_done, FT * b + t + 1)
                elif name == "up":
                    pe.wait_ge(h_ready, FT * b + t + 1)
                elif name == "wo":
                    pe.wait_ge(x1_ready, TT * (b + ahead) + t + 1)
                else:
                    pe.wait_ge(xt_ready, KC * (b + ahead) + t + 1)

            def project_out(b, t, units, at):
                unit = units["wo", t]
                pe.wait_ge(ctx_lo_ready, TT * b + t + 1)
                wait_bank(unit, units, at)
                three_products(bank[unit % BANKS][:], lambda w, c: ctx_t[w][:, c, :], lambda m, c: wo[m][:, c, :],
                               KC).then_inc(wo_done, 1)

            def transposed_x(b, kc, units, at):
                unit = units["T", kc]
                pe.wait_ge(xn_ready, TT * (b + 1))
                wait_bank(unit, units, at)
                for t in range(TT):
                    mm = nc.tensor.transpose(bank[unit % BANKS][:, P * t:P * (t + 1)],
                                             xn[:, t, P * kc:P * (kc + 1)], ident[:])
                mm.then_inc(xt_done, 1)

            def down(b, f):
                n, m, r = FT * b + f, FW[f], f % 2
                pe.wait_ge(h_lo_ready, n + 1)
                if f == 0 and (not isinstance(b, int) or b > 0):
                    pe.wait_ge(y_evacuated, TT * b)
                for t in range(TT):
                    for k, (w, p) in enumerate(PRODUCTS):
                        mm = nc.tensor.matmul(ps_y[:, t], h_parts[w][0:m, r, P * t:P * (t + 1)], wd[p][0:m, f, :],
                                              start=(f == 0 and k == 0), stop=(f == FT - 1 and k == 2))
                mm.then_inc(down_done, 1)

            def iteration(b, has_next):
                units = RING_FULL if has_next else RING_LAST
                first = isinstance(b, int) and b == 0
                pe.wait_ge(xt_ready, KC * (b + 1))
                for f in range(FT):
                    m = FW[f]
                    if first:
                        pe.wait_ge(ffn_split, 3 * (f + 1))
                    for name, w, ready in (("gate", wg, gate_ready), ("up", wu, up_ready)):
                        unit = units[name, f]
                        wait_bank(unit, units, b)
                        three_products(bank[unit % BANKS][0:m, :], lambda q, c: w[q][:, c, P * f:P * f + m],
                                       lambda q, c: xt[q][:, c, :], KC).then_inc(ready, 1)
                    if has_next and 0 <= f - WO_SLOT < TT:
                        project_out(b + 1, f - WO_SLOT, units, b)
                    if f >= 1:
                        down(b, f - 1)
                if has_next:
                    for kc in range(KC):
                        transposed_x(b + 1, kc, units, b)
                down(b, FT - 1)

            pe.wait_ge(ident_ready, 1)
            pe.wait_ge(wo_split, KC)
            for t in range(TT):
                project_out(0, t, RING_PRE, 0)
            for kc in range(KC):
                transposed_x(0, kc, RING_PRE, 0)
            iteration(0, True)
            with pe.Fori(1, B - 1) as b:
                iteration(b, True)
            iteration(B - 1, False)


def build(nc, d):
    phase_1(nc, d)
    phase_2(nc, d)


def rope_tables():
    import numpy as np
    f = np.float32
    theta, factor, lo, hi, length = 500000.0, 32.0, 1.0, 4.0, 1024
    at = np.arange(0, DH, 2, dtype=f) / f(DH)
    freq = f(1.0 / (2.0 * np.pi)) * np.power(f(theta), -at)
    low, high = f(lo / length), f(hi / length)
    scaled = np.where(freq < low, freq / f(factor), freq)
    smooth = np.clip((f(length) * freq - f(lo)) / f(hi - lo), f(0), f(1))
    blended = (f(1) - smooth) * (freq / f(factor)) + smooth * freq
    freq = np.where((freq >= low) & (freq <= high), blended, scaled).astype(f)
    phase = f(2.0 * np.pi) * np.arange(T, dtype=f)[None, :] * freq[:, None]
    cos, sin = np.cos(phase), np.sin(phase)
    heads = P // DH
    return (np.tile(np.concatenate([cos, cos]), (heads, 1)).astype(f),
            np.tile(np.concatenate([-sin, sin]), (heads, 1)).astype(f))


def kernel(L0_attn_resid, L0_attn_Wq, L0_attn_Wk, L0_attn_Wv, L0_attn_Wo, L0_ffn_W_gate, L0_ffn_W_up,
           L0_ffn_W_down):
    import numpy as np
    import concourse.bacc as bacc
    from concourse.bass_utils import run_bass_kernel_spmd

    nc = bacc.Bacc("TRN2", target_bir_lowering=False, num_devices=1)
    cos, sin = rope_tables()
    given = {"x": L0_attn_resid, "wq": L0_attn_Wq, "wk": L0_attn_Wk, "wv": L0_attn_Wv, "wo": L0_attn_Wo,
             "wg": np.asarray(L0_ffn_W_gate).T, "wu": np.asarray(L0_ffn_W_up).T,
             "wd": np.asarray(L0_ffn_W_down).T, "cos": cos, "sin": sin}
    arrays, d = {}, {}
    for name, a in given.items():
        a = np.ascontiguousarray(a)
        arrays[f"in_{name}"] = a
        d[name] = nc.dram_tensor(f"in_{name}", a.shape, F32, kind="ExternalInput").ap()
    for name, shape in (("q_parts", (B, D // DH, 3, DH, T)), ("k_parts", (B, NKV, 3, DH, T)),
                        ("o", (B, NKV, P, T)), ("x1", (B, T, D)), ("wo_raw", (D, D)), ("wg_raw", (D, F)),
                        ("wu_raw", (D, F)), ("wd_raw", (F, D))):
        d[name] = nc.dram_tensor(f"scratch_{name}", shape, F32, kind="Internal").ap()
    d["out"] = nc.dram_tensor("out", (B, T, D), F32, kind="ExternalOutput").ap()
    build(nc, d)
    r = run_bass_kernel_spmd(nc, [arrays], core_ids=[0])
    return r.results[0]["out"]
```

```python
from contextlib import ExitStack

import concourse.bass as bass
from concourse import mybir

F32 = mybir.dt.float32
F32R = mybir.dt.float32r
BF16 = mybir.dt.bfloat16
AXIS = mybir.AxisListType
ALU = mybir.AluOpType
ACT = mybir.ActivationFunctionType

P = 128
B, T, D = 4, 512, 512
NKV, GROUP, DH = 8, 4, 16
F = 1376
TT, KC = T // P, D // P
QT = D // P
KVW = NKV * DH
FT = -(-F // P)
FW = [min(P, F - P * f) for f in range(FT)]
SCALE = float(DH) ** -0.5
EPS = 1e-5
MASKED = -1.0e30
CHUNK_N = [T - P * c for c in range(TT)]
CHUNK_AT = [sum(CHUNK_N[:c]) for c in range(TT + 1)]
HEADS_OF = [2 if 2 * n <= T else 1 for n in CHUNK_N]
BANK_AT = [sum(GROUP // h for h in HEADS_OF[:i]) for i in range(TT + 1)]
BANKS_OF = BANK_AT[TT]
S_BANKS = 3
ROWS = 3 * DH
PAIR = 2 * ROWS
PAIR_M = PAIR + 2
RING = 4
DMA = 16

MAX_AFTER = 3
PV_AFTER = (2, 2, 2, 3)
T_AFTER = 3
PIECE_AFTER = ((0, 1, 2, 3), (2, 2, 3, 3), (0, 1, 2, 3), (2, 3, 3, 3))
STATS_SLOT, MEAN_SLOT, APPLY_SLOT = 2, 4, 5
UNIT_SLOT = {7: ("T", 0), 9: ("T", 1), 10: ("T", 2), 11: ("T", 3), 13: ("R", 0), 15: ("R", 1),
             18: ("R", 2), 21: ("V", 0), 23: ("R", 3), 26: ("R", 4)}
SUMS_SLOT, INVERSE_SLOT = 2, 8
WO_LOAD, RESIDUAL_LOAD, O_LOAD, WO_HI, WO_LO = 10, 14, (18, 20, 25), 14, 18
SCALE_SLOTS, CTX_HI, CTX_LO = (22, 26), 23, 24
HI_AFTER, LO_AFTER = 3, 4
N_ROPE = 1 + QT


def unit_numbers(slots):
    number, n = {}, 0
    for s in range(TT * NKV):
        if s % TT == 0:
            number[s] = n
            n += 1
        elif s in slots:
            number[s] = n
            n += 1
    return number, n


UNIT_NO, UNITS = unit_numbers(UNIT_SLOT)
PRE_DENSE = KC + N_ROPE + 1
PRE_UNITS = PRE_DENSE + 1
PRE_BANKS = 1 + S_BANKS


def positive(count):
    return not isinstance(count, int) or count > 0


class Handover:

    def __init__(self, nc, ctx):
        def sb(name, shape, dt=F32):
            return ctx.enter_context(nc.sbuf_tensor(name, shape, dt))

        def sem(name):
            return ctx.enter_context(nc.semaphore(name))

        self.wo = [sb(f"wo_{p}", [P, KC, D], F32R) for p in ("hi", "lo")]
        self.o_in = sb("o_in", [P, 2, QT, P])
        self.inverse = sb("inverse", [P, 2, QT, P])
        self.x_res = sb("x_res", [P, 2, D])
        self.ident = sb("ident", [P, P])
        self.ctx = [sb(f"ctx_{p}", [P, QT, P], F32R) for p in ("hi", "lo")]
        self.ctx_scaled = sem("ctx_scaled")
        self.ctx_hi_ready = sem("ctx_hi_ready")
        self.ctx_lo_ready = sem("ctx_lo_ready")
        self.wo_loaded = sem("wo_loaded")
        self.wo_hi_ready = sem("wo_hi_ready")
        self.wo_split = sem("wo_split")
        self.o_loaded = [sem(f"o_loaded{r}") for r in range(2)]
        self.xres_loaded = [sem(f"xres_loaded{r}") for r in range(2)]


def load_o(sp, d, to, b, t):
    o = d["o"][b].rearrange("g (j s w) t -> s (g j) w t", j=GROUP, s=2)[0]
    for c in range(KC):
        heads, at = slice(P // DH * c, P // DH * (c + 1)), slice(P * t, P * (t + 1))
        sp.dma_start(to.o_in[:, t % 2, c], o[heads, :, at]).then_inc(to.o_loaded[t % 2], DMA)
        sp.dma_start(to.inverse[:, t % 2, c], d["inverse"][b, heads, at].unsqueeze(1).broadcast_to(
            [P // DH, DH, P])).then_inc(to.o_loaded[t % 2], DMA)


def load_residual(sp, d, to, b, t):
    sp.dma_start(to.x_res[:, t % 2], d["x"][b, P * t:P * (t + 1)]).then_inc(to.xres_loaded[t % 2], DMA)


def scale_ctx(dve, to, b, t):
    r = t % 2
    dve.wait_ge(to.o_loaded[r], 2 * KC * DMA * (TT // 2 * b + t // 2 + 1))
    dve.tensor_tensor(to.o_in[:, r], to.o_in[:, r], to.inverse[:, r], ALU.mult).then_inc(to.ctx_scaled, 1)


def ctx_high(act, to, b, t, parts):
    act.wait_ge(to.ctx_scaled, TT * b + t + 1)
    act.copy(parts[0][:], to.o_in[:, t % 2]).then_inc(to.ctx_hi_ready, 1)


def ctx_low(dve, to, b, t, parts):
    dve.wait_ge(to.ctx_hi_ready, TT * b + t + 1)
    dve.tensor_tensor(parts[1][:], to.o_in[:, t % 2], parts[0][:].bitcast(F32), ALU.subtract
                      ).then_inc(to.ctx_lo_ready, 1)


def row_sums(d, b):
    return d["o"][b].rearrange("g (j s w) (k t) -> s w (g j) k t", j=GROUP, s=2, k=TT)[1, 0]


def row_inverses(d, b):
    return d["inverse"][b].rearrange("h (k t) -> (h k) t", k=TT)


def phase_1(nc, d, to):
    with ExitStack() as ctx:
        def sb(name, shape, dt=F32):
            return ctx.enter_context(nc.sbuf_tensor(name, shape, dt))

        def psum(name, shape):
            return ctx.enter_context(nc.psum_tensor(name, shape, F32))

        def sem(name):
            return ctx.enter_context(nc.semaphore(name))

        ident = to.ident
        ident_b = sb("ident_b", [P, P], BF16)
        mask_q = sb("mask_q", [P, 2, P], BF16)
        mask_k = sb("mask_k", [P, 2, P], BF16)
        half = sb("half", [P, TT])
        eps = sb("eps", [P, TT])
        cos = sb("cos", [P, T])
        sin = sb("sin", [P, T])
        w_hi = sb("w_hi", [P, KC, D + 2 * KVW], F32R)
        w_lo = sb("w_lo", [P, KC, D + 2 * KVW], F32R)
        x_in = sb("x_in", [P, TT, D])
        stats = sb("stats", [P, TT, 6])
        mean_var = sb("mean_var", [P, TT, 2])
        var_eps = sb("var_eps", [P, TT])
        rstd = sb("rstd", [P, TT])
        xn = sb("xn", [P, TT, D])
        xt_hi = sb("xt_hi", [P, KC, T], F32R)
        xt_lo = sb("xt_lo", [P, KC, T], F32R)
        rot_c = sb("rot_c", [P, 2, T])
        rot_s = sb("rot_s", [P, 2, T])
        r_hi = sb("r_hi", [P, 2, T], F32R)
        r_lo = sb("r_lo", [P, 2, T], F32R)
        v_next = sb("v_next", [P, TT, KVW])
        v_ones = sb("v_ones", [P, TT, NKV, 2 * DH])
        q_rows = [sb(f"q_rows{r}", [PAIR_M, GROUP, T]) for r in range(RING)]
        k_rows = [sb(f"k_rows{r}", [PAIR_M, T]) for r in range(RING)]
        m_raw = sb("m_raw", [P, 2, TT * GROUP])
        m_parts = sb("m_parts", [P, 2, TT, 2, GROUP])
        m_t = [sb(f"m_t{r}", [2 * GROUP, T]) for r in range(2)]
        probs = sb("probs", [P, 2, GROUP, CHUNK_AT[TT]])
        o_sb = sb("o_sb", [P, 2, T])
        sums = sb("sums", [P, P])
        w_raw = probs[:].rearrange("p r j t -> p (r j t)")[:, 0:KC * (D + 2 * KVW)].rearrange("p (c n) -> p c n", c=KC)

        ps_s = psum("ps_s", [P, S_BANKS, T])
        ps_t = psum("ps_t", [P, S_BANKS, T])
        ps_o = psum("ps_o", [P, T])
        ps_d = psum("ps_d", [P, T])

        def dense_bank(unit):
            if isinstance(unit, int) and unit < PRE_DENSE and unit % PRE_BANKS:
                return ps_t[:, unit % PRE_BANKS - 1]
            return ps_d[:]

        consts_ready = sem("consts_ready")
        const_step = sem("const_step")
        rows_cleared = sem("rows_cleared")
        tables_loaded = sem("tables_loaded")
        w_loaded = sem("w_loaded")
        w_hi_ready = sem("w_hi_ready")
        w_split = sem("w_split")
        raw_copied = sem("raw_copied")
        x_loaded = [sem(f"x_loaded{t}") for t in range(TT)]
        ln_stats = sem("ln_stats")
        ln_mean = sem("ln_mean")
        var_ready = sem("var_ready")
        rstd_ready = sem("rstd_ready")
        xn_ready = sem("xn_ready")
        dense_ready = sem("dense_ready")
        dense_evacuated = sem("dense_evacuated")
        xt_hi_ready = sem("xt_hi_ready")
        rope_sin = sem("rope_sin")
        rope_done = sem("rope_done")
        r_hi_ready = sem("r_hi_ready")
        r_lo_ready = sem("r_lo_ready")
        r_stored = [sem(f"r_stored{k}") for k in range(N_ROPE)]
        v_ready = sem("v_ready")
        rows_staged = [sem(f"rows_staged{r}") for r in range(RING)]
        scores_ready = sem("scores_ready")
        max_done = sem("max_done")
        m_hi_ready = sem("m_hi_ready")
        m_split = sem("m_split")
        m_staged = [sem(f"m_staged{r}") for r in range(2)]
        scores_t_ready = sem("scores_t_ready")
        exp_done = sem("exp_done")
        pv_done = sem("pv_done")
        o_evacuated = sem("o_evacuated")
        sums_loaded = sem("sums_loaded")
        inverse_ready = sem("inverse_ready")
        inverse_stored = sem("inverse_stored")
        o_stored = [sem(f"o_stored{r}") for r in range(2)]

        R_STORE = 3 * DMA
        ROW_DMAS = 4 * DMA

        block = ctx.enter_context(nc.Block())

        @block.sync
        def _(sp):
            def load_x(b):
                for t in range(TT):
                    sp.dma_start(x_in[:, t], d["x"][b, P * t:P * (t + 1)]).then_inc(x_loaded[t], DMA)

            load_x(0)
            for at, name, width in ((0, "wq", D), (D, "wk", KVW), (D + KVW, "wv", KVW)):
                sp.dma_start(w_raw[:, :, at:at + width],
                             d[name].rearrange("(c p) n -> p c n", p=P)).then_inc(w_loaded, DMA)
            sp.dma_start(cos[:], d["cos"]).then_inc(tables_loaded, DMA)
            sp.dma_start(sin[:], d["sin"]).then_inc(tables_loaded, DMA)
            sp.dma_start(d["wo_raw"], d["wo"]).then_inc(raw_copied, DMA)

            def copy_raw(n):
                name = ("wg", "wu", "wd")[n // 4]
                rows = d[name].shape[0] // 4
                at = slice(rows * (n % 4), rows * (n % 4 + 1))
                sp.dma_start(d[name + "_raw"][at], d[name][at]).then_inc(raw_copied, DMA)

            def store_rotated(b, k):
                sp.wait_ge(r_lo_ready, N_ROPE * b + k + 1)
                to = d["k_parts"][b] if k == 0 else d["q_parts"][b, P // DH * (k - 1):P // DH * k]
                for part, tile in enumerate((r_hi, r_lo, r_hi) if k == 0 else (r_hi, r_hi, r_lo)):
                    sp.dma_start(to[:, part], tile[:, k % 2, :].bitcast(F32)).then_inc(r_stored[k], DMA)

            def stage_rows(b, g, n):
                used = BANKS_OF * (n - RING + 1)
                if not isinstance(used, int):
                    sp.compute_val(used)
                if g == 0:
                    sp.wait_ge(r_stored[0], R_STORE * (b + 1))
                if g % 2 == 0:
                    sp.wait_ge(r_stored[1 + g // 2], R_STORE * (b + 1))
                if positive(used):
                    sp.wait_ge(scores_t_ready, used)
                r = g % RING
                heads = d["q_parts"][b, GROUP * g:GROUP * (g + 1)].rearrange("(i s) p w t -> s (p w) i t", s=2)
                for s in range(2):
                    sp.dma_start(q_rows[r][ROWS * s:ROWS * (s + 1), s:GROUP:2, :], heads[s]
                                 ).then_inc(rows_staged[r], DMA)
                for s in range(2):
                    sp.dma_start(k_rows[r][ROWS * s:ROWS * (s + 1), :],
                                 d["k_parts"][b, g].rearrange("p w t -> (p w) t")).then_inc(rows_staged[r], DMA)

            def stage_max(g, unit):
                sp.wait_ge(dense_evacuated, unit + 1)
                sp.dma_start(q_rows[g % RING][PAIR:PAIR_M], m_t[g % 2][:]).then_inc(m_staged[g % 2], DMA)

            def store_o(b, g):
                sp.wait_ge(o_evacuated, NKV * b + g + 1)
                sp.dma_start(d["o"][b, g], o_sb[:, g % 2, :]).then_inc(o_stored[g % 2], DMA)

            def load_sums(b):
                for stored in o_stored:
                    sp.wait_ge(stored, DMA * NKV // 2 * (b + 1))
                sp.dma_start(sums[:], row_sums(d, b)).then_inc(sums_loaded, DMA)

            def store_inverse(b):
                sp.wait_ge(inverse_ready, b + 1)
                sp.dma_start(row_inverses(d, b), sums[:]).then_inc(inverse_stored, DMA)

            def prepare_phase_2(slot):
                if slot == WO_LOAD:
                    sp.wait_ge(raw_copied, 13 * DMA)
                    sp.dma_start(to.wo[1][:].bitcast(F32), d["wo_raw"].rearrange("(c p) n -> p c n", p=P)
                                 ).then_inc(to.wo_loaded, DMA)
                if slot == RESIDUAL_LOAD:
                    load_residual(sp, d, to, 0, 0)
                    load_residual(sp, d, to, 0, 1)
                if slot in O_LOAD:
                    t = O_LOAD.index(slot)
                    if t == 0:
                        sp.wait_ge(inverse_stored, (B - 1) * DMA)
                    if t == 2:
                        sp.wait_ge(to.ctx_lo_ready, 1)
                    load_o(sp, d, to, 0, t)

            def iteration(b, has_next):
                if has_next:
                    sp.wait_ge(xn_ready, TT * (b + 1))
                    load_x(b + 1)
                for slot in range(TT * NKV):
                    g, i = slot // TT, slot % TT
                    unit0 = UNITS * b + PRE_UNITS
                    if i == 1 and (has_next or g < NKV - 1):
                        stage_max(g + 1, unit0 + (UNIT_NO[slot - 1] if has_next else g))
                    if i == 1 and g >= 1:
                        store_o(b, g - 1)
                    if has_next and UNIT_SLOT.get(slot - LO_AFTER, "-")[0] == "R":
                        store_rotated(b + 1, UNIT_SLOT[slot - LO_AFTER][1])
                    if i == 1 and g + 3 < NKV:
                        stage_rows(b, g + 3, NKV * b + g + 3)
                    if i == 1 and g + 3 >= NKV and has_next:
                        stage_rows(b + 1, g + 3 - NKV, NKV * b + g + 3)
                    if not positive(b) and i >= 2 and g < 6:
                        copy_raw(2 * g + i - 2)
                    if positive(b) and slot == SUMS_SLOT:
                        load_sums(b - 1)
                    if positive(b) and slot == INVERSE_SLOT + 1:
                        store_inverse(b - 1)
                    if not has_next:
                        prepare_phase_2(slot)
                store_o(b, NKV - 1)

            sp.wait_ge(rows_cleared, 2 * RING)
            for k in range(3):
                store_rotated(0, k)
            stage_rows(0, 0, 0)
            stage_rows(0, 1, 1)
            store_rotated(0, 3)
            stage_rows(0, 2, 2)
            store_rotated(0, 4)
            stage_max(0, PRE_UNITS - 1)
            iteration(0, True)
            with sp.Fori(1, B - 1) as b:
                iteration(b, True)
            iteration(B - 1, False)
            for stored in o_stored:
                sp.wait_ge(stored, DMA * NKV // 2 * B)
            for stored in r_stored:
                sp.wait_ge(stored, R_STORE * B)

        @block.gpsimd
        def _(pool):
            pool.memset(half[:], -0.5)
            pool.memset(eps[:], EPS)
            pool.memset(v_ones[:], 1.0)
            pool.memset(ident[:], 0.0)
            pool.memset(ident_b[:], 0.0)
            pool.memset(mask_q[:], 0.0)
            pool.memset(mask_k[:], 0.0).then_inc(const_step, 1)
            pool.wait_ge(const_step, 1)
            for tile in (ident, ident_b):
                nc.gpsimd.affine_select(out=tile[:], in_=tile[:], compare_op=ALU.not_equal, fill=1.0, base=0,
                                        pattern=[[-1, P]], channel_multiplier=1)
            nc.gpsimd.affine_select(out=mask_q[:], in_=mask_q[:], compare_op=ALU.is_ge, fill=MASKED, base=0,
                                    pattern=[[0, 2], [-1, P]], channel_multiplier=1)
            nc.gpsimd.affine_select(out=mask_k[:], in_=mask_k[:], compare_op=ALU.is_ge, fill=MASKED, base=0,
                                    pattern=[[0, 2], [1, P]], channel_multiplier=-1).then_inc(consts_ready, 1)
            pool.wait_ge(consts_ready, 1)
            def layernorm_scale(b):
                pool.wait_ge(ln_mean, TT * (b + 1))
                nc.gpsimd.tensor_tensor(var_eps[:], mean_var[:, :, 1], eps[:], ALU.add).then_inc(var_ready, 1)
                pool.wait_ge(var_ready, b + 1)
                nc.gpsimd.tensor_tensor(rstd[:], var_eps[:], half[:], ALU.pow).then_inc(rstd_ready, 1)

            def rotate(b, k, unit):
                r = k % 2
                pool.wait_ge(dense_evacuated, unit + 1)
                nc.gpsimd.tensor_tensor(rot_s[:, r], rot_s[:, r], sin[:], ALU.mult).then_inc(rope_sin, 1)
                pool.wait_ge(rope_sin, N_ROPE * b + k + 1)
                nc.gpsimd.tensor_tensor(rot_c[:, r], rot_c[:, r], rot_s[:, r], ALU.add).then_inc(rope_done, 1)

            layernorm_scale(0)
            for r in range(RING):
                pool.memset(q_rows[r][0:PAIR], 0.0).then_inc(rows_cleared, 1)
            pool.wait_ge(tables_loaded, 2 * DMA)
            for k in range(N_ROPE):
                rotate(0, k, KC + k)
            with pool.Fori(0, B - 1) as b:
                layernorm_scale(b + 1)
                for slot, (kind, k) in UNIT_SLOT.items():
                    if kind == "R":
                        rotate(b + 1, k, UNITS * b + PRE_UNITS + UNIT_NO[slot])

        @block.scalar
        def _(act):
            def xt_high(unit, kc):
                act.wait_ge(dense_ready, unit + 1)
                nc.scalar.copy(xt_hi[:, kc], dense_bank(unit)).then_inc(xt_hi_ready, 1)

            def rotated_high(b, k):
                act.wait_ge(rope_done, N_ROPE * b + k + 1)
                if k >= 2:
                    act.wait_ge(r_stored[k - 2], R_STORE * (b + 1))
                elif not isinstance(b, int):
                    act.wait_ge(r_stored[N_ROPE - 1 - k], R_STORE * b)
                nc.scalar.copy(r_hi[:, k % 2], rot_c[:, k % 2]).then_inc(r_hi_ready, 1)

            def v_evacuate(unit):
                act.wait_ge(dense_ready, unit + 1)
                act.wait_ge(dense_evacuated, unit)
                nc.scalar.copy(v_next[:].rearrange("p t n -> p (t n)"), dense_bank(unit)).then_inc(dense_evacuated, 1)

            def v_place(b, unit):
                act.wait_ge(dense_evacuated, unit + 1)
                nc.scalar.copy(v_ones[:, :, :, 0:DH].rearrange("p t h w -> p (t h) w"),
                               v_next[:].rearrange("p t (h w) -> p (t h) w", w=DH)).then_inc(v_ready, 1)

            def max_evacuate(b, g, unit):
                act.wait_ge(dense_ready, unit + 1)
                if not isinstance(b, int) or b >= 1 or g >= 2:
                    act.wait_ge(m_staged[g % 2], DMA * (NKV // 2 * b + g // 2))
                nc.scalar.copy(m_t[g % 2][:], ps_d[0:2 * GROUP, :]).then_inc(dense_evacuated, 1)

            def exponentials(b, g, c):
                heads = HEADS_OF[c]
                for u in range(GROUP // heads):
                    n = BANKS_OF * (NKV * b + g) + BANK_AT[c] + u
                    if c == 0 and u == 0:
                        if positive(NKV * b + max(g - 1, 0)):
                            act.wait_ge(pv_done, NKV * b + max(g - 1, 0))
                    act.wait_ge(scores_t_ready, n + 1)
                    nc.scalar.activation(
                        probs[:, g % 2, heads * u:heads * (u + 1), CHUNK_AT[c]:CHUNK_AT[c + 1]],
                        ps_t[:, (BANK_AT[c] + u) % S_BANKS, 0:heads * CHUNK_N[c]].rearrange("p (j t) -> p j t", j=heads),
                        ACT.Exp, scale=SCALE).then_inc(exp_done, 1)

            def o_evacuate(b, g):
                act.wait_ge(pv_done, NKV * b + g + 1)
                if positive(NKV // 2 * b + g // 2):
                    act.wait_ge(o_stored[g % 2], DMA * (NKV // 2 * b + g // 2))
                nc.scalar.copy(o_sb[:, g % 2], ps_o[:]).then_inc(o_evacuated, 1)

            def iteration(b, has_next):
                unit0 = UNITS * b + PRE_UNITS
                for slot in range(TT * NKV):
                    g, i = slot // TT, slot % TT
                    kind, k = UNIT_SLOT.get(slot - 1, "--")
                    if has_next and kind == "T":
                        xt_high(unit0 + UNIT_NO[slot - 1], k)
                    if has_next and kind == "V":
                        v_evacuate(unit0 + UNIT_NO[slot - 1])
                    if i == 1 and g >= 1:
                        o_evacuate(b, g - 1)
                    if i == 1 and (has_next or g < NKV - 1):
                        max_evacuate(b, g + 1, unit0 + (UNIT_NO[slot - 1] if has_next else g))
                    exponentials(b, g, i)
                    kind, k = UNIT_SLOT.get(slot - HI_AFTER, "--")
                    if has_next and kind == "R":
                        rotated_high(b + 1, k)
                    if not has_next and slot == CTX_HI:
                        ctx_high(act, to, 0, 0, to.ctx)
                    if not has_next and WO_HI <= slot < WO_HI + KC:
                        c = slot - WO_HI
                        act.wait_ge(to.wo_loaded, DMA)
                        nc.scalar.copy(to.wo[0][:, c], to.wo[1][:, c].bitcast(F32)).then_inc(to.wo_hi_ready, 1)
                o_evacuate(b, NKV - 1)
                if has_next:
                    v_place(b, unit0 + UNIT_NO[[s for s, u in UNIT_SLOT.items() if u[0] == "V"][0]])

            act.wait_ge(w_loaded, 3 * DMA)
            for c in range(KC):
                nc.scalar.copy(w_hi[:, c], w_raw[:, c]).then_inc(w_hi_ready, 1)
            for kc in range(KC):
                xt_high(kc, kc)
            for k in range(N_ROPE):
                rotated_high(0, k)
            v_evacuate(KC + N_ROPE)
            act.wait_ge(consts_ready, 1)
            v_place(0, KC + N_ROPE)
            max_evacuate(0, 0, PRE_UNITS - 1)
            iteration(0, True)
            with act.Fori(1, B - 1) as b:
                iteration(b, True)
            iteration(B - 1, False)

        @block.vector
        def _(dve):
            swap = [(p + DH // 2) % DH + DH * (p // DH) for p in range(32)]

            def layernorm_stats(b, t):
                dve.wait_ge(x_loaded[t], DMA * (b + 1))
                nc.vector.bn_stats(stats[:, t], x_in[:, t]).then_inc(ln_stats, 1)

            def layernorm_mean():
                for t in range(TT):
                    nc.vector.bn_aggr(mean_var[:, t], stats[:, t]).then_inc(ln_mean, 1)

            def layernorm_apply(b, t):
                dve.wait_ge(rstd_ready, b + 1)
                nc.vector.tensor_scalar(xn[:, t], x_in[:, t], mean_var[:, t, 0:1], rstd[:, t:t + 1],
                                        ALU.subtract, ALU.mult).then_inc(xn_ready, 1)

            def xt_low(b, kc, unit):
                dve.wait_ge(xt_hi_ready, KC * b + kc + 1)
                nc.vector.tensor_tensor(xt_lo[:, kc], dense_bank(unit), xt_hi[:, kc].bitcast(F32),
                                        ALU.subtract).then_inc(dense_evacuated, 1)

            def rope_cos(b, k, unit):
                r = k % 2
                if k >= 2:
                    dve.wait_ge(r_lo_ready, N_ROPE * b + k - 1)
                elif positive(b):
                    dve.wait_ge(r_lo_ready, N_ROPE * b)
                dve.wait_ge(dense_ready, unit + 1)
                nc.vector.tensor_tensor(rot_c[:, r], dense_bank(unit), cos[:], ALU.mult)

            def rope_swap(k, unit):
                nc.vector.stream_shuffle(rot_s[:, k % 2], dense_bank(unit), swap).then_inc(dense_evacuated, 1)

            def rotated_low(b, k):
                r = k % 2
                dve.wait_ge(r_hi_ready, N_ROPE * b + k + 1)
                nc.vector.tensor_tensor(r_lo[:, r], rot_c[:, r], r_hi[:, r].bitcast(F32),
                                        ALU.subtract).then_inc(r_lo_ready, 1)

            def row_max(n, g, i, between=()):
                heads, width = HEADS_OF[i], CHUNK_N[i]
                for u in range(GROUP // heads):
                    at = GROUP * (TT - 1 - i) + heads * u
                    dve.wait_ge(scores_ready, BANKS_OF * n + BANK_AT[i] + u + 1)
                    nc.vector.tensor_reduce(
                        out=m_raw[:, g % 2, at:at + heads], op=ALU.max, axis=AXIS.X,
                        in_=ps_s[:, (BANK_AT[i] + u) % S_BANKS, 0:heads * width].rearrange("p (j t) -> p j t", j=heads)
                    ).then_inc(max_done, 1)
                    if u < len(between):
                        between[u]()

            def split_max(n, g):
                r = g % 2
                raw = m_raw[:, r, :].rearrange("p (q j) -> p q j", j=GROUP)
                hi = m_parts[:, r, :, 0, :]
                lo = m_parts[:, r, :, 1, :]
                dve.wait_ge(max_done, BANKS_OF * (n + 1))
                nc.vector.tensor_copy(hi.bitcast(F32R), raw).then_inc(m_hi_ready, 1)
                dve.wait_ge(m_hi_ready, n + 1)
                nc.vector.tensor_tensor(lo.bitcast(F32R), raw, hi, ALU.subtract).then_inc(m_split, 1)

            def invert_sums(b):
                dve.wait_ge(sums_loaded, DMA * (b + 1))
                if positive(b):
                    dve.wait_ge(inverse_stored, DMA * b)
                nc.vector.reciprocal(sums[:], sums[:]).then_inc(inverse_ready, 1)

            def split_wo(c):
                dve.wait_ge(to.wo_hi_ready, c + 1)
                nc.vector.tensor_tensor(to.wo[1][:, c], to.wo[1][:, c].bitcast(F32), to.wo[0][:, c].bitcast(F32),
                                        ALU.subtract).then_inc(to.wo_split, 1)

            def other_work(b, slot, unit0):
                work = []
                kind, k = UNIT_SLOT.get(slot - 1, "--")
                if kind == "T":
                    work.append(lambda: xt_low(b + 1, k, unit0 + UNIT_NO[slot - 1]))
                elif kind == "R":
                    work += [lambda: rope_cos(b + 1, k, unit0 + UNIT_NO[slot - 1]), lambda: rope_swap(k, unit0 + UNIT_NO[slot - 1])]
                kind, split = UNIT_SLOT.get(slot - LO_AFTER, "--")
                if kind == "R":
                    work.append(lambda: rotated_low(b + 1, split))
                if slot == MEAN_SLOT:
                    work.append(layernorm_mean)
                for at, step in ((STATS_SLOT, layernorm_stats), (APPLY_SLOT, layernorm_apply)):
                    if 0 <= slot - at < TT // 2:
                        for t in range(2 * (slot - at), 2 * (slot - at) + 2):
                            work.append(lambda step=step, t=t: step(b + 1, t))
                return work

            def iteration(b, has_next):
                unit0 = UNITS * b + PRE_UNITS
                for slot in range(TT * NKV):
                    g, i = slot // TT, slot % TT
                    if has_next and slot == MEAN_SLOT:
                        dve.wait_ge(ln_stats, TT * (b + 2))
                    others = other_work(b, slot, unit0) if has_next else []
                    if positive(b) and slot == INVERSE_SLOT:
                        others.append(lambda: invert_sums(b - 1))
                    if not has_next and WO_LO <= slot < WO_LO + KC:
                        others.append(lambda: split_wo(slot - WO_LO))
                    if not has_next and slot == CTX_LO:
                        others.append(lambda: ctx_low(dve, to, 0, 0, to.ctx))
                    if not has_next and slot in SCALE_SLOTS:
                        others.append(lambda: scale_ctx(dve, to, 0, SCALE_SLOTS.index(slot)))
                    if has_next or g < NKV - 2:
                        row_max(NKV * b + g + 2, g, i, others)
                        others = others[GROUP // HEADS_OF[i]:]
                        if i == TT - 1:
                            split_max(NKV * b + g + 2, g)
                    for work in others:
                        work()

            for r in range(RING):
                nc.vector.memset(k_rows[r][PAIR:PAIR_M], -1.0).then_inc(rows_cleared, 1)
            for t in range(TT):
                layernorm_stats(0, t)
            dve.wait_ge(ln_stats, TT)
            layernorm_mean()
            for t in range(TT):
                layernorm_apply(0, t)
            for c in range(KC):
                dve.wait_ge(w_hi_ready, c + 1)
                nc.vector.tensor_tensor(w_lo[:, c], w_raw[:, c], w_hi[:, c].bitcast(F32),
                                        ALU.subtract).then_inc(w_split, 1)
            for kc in range(KC):
                xt_low(0, kc, kc)
            dve.wait_ge(tables_loaded, 2 * DMA)
            for k in range(N_ROPE):
                if k >= 2:
                    rotated_low(0, k - 2)
                rope_cos(0, k, KC + k)
                rope_swap(k, KC + k)
            dve.wait_ge(consts_ready, 1)
            row_max(0, 0, 0, [lambda: rotated_low(0, N_ROPE - 2), lambda: rotated_low(0, N_ROPE - 1)])
            for i in range(1, TT):
                row_max(0, 0, i)
            split_max(0, 0)
            for i in range(TT):
                row_max(1, 1, i)
            split_max(1, 1)
            iteration(0, True)
            with dve.Fori(1, B - 1) as b:
                iteration(b, True)
            iteration(B - 1, False)

        @block.tensor
        def _(pe):
            PRODUCTS = ((0, 0), (0, 1), (1, 0))
            W, X = (w_hi, w_lo), (xt_hi, xt_lo)

            def bank_free(unit, piece):
                read = unit - PRE_BANKS + 1 if isinstance(unit, int) and unit < PRE_DENSE else unit
                if piece == 0 and positive(read):
                    pe.wait_ge(dense_evacuated, read)

            def transposed_x(b, kc, unit, t):
                if t == 0:
                    pe.wait_ge(xn_ready, TT * (b + 1))
                bank_free(unit, t)
                mm = nc.tensor.transpose(dense_bank(unit)[:, P * t:P * (t + 1)], xn[:, t, P * kc:P * (kc + 1)], ident[:])
                if t == TT - 1:
                    mm.then_inc(dense_ready, 1)

            def project(k, unit, c):
                at = D if k == 0 else P * (k - 1)
                if k == 0 and c == 0:
                    pe.wait_ge(dense_evacuated, unit)
                bank_free(unit, c)
                for n, (w, x) in enumerate(PRODUCTS):
                    mm = nc.tensor.matmul(dense_bank(unit), W[w][:, c, at:at + P], X[x][:, c, :], start=(c == 0 and n == 0),
                                          stop=(c == KC - 1 and n == 2))
                if c == KC - 1:
                    mm.then_inc(dense_ready, 1)

            def project_v(unit, t):
                bank_free(unit, t)
                for c in range(KC):
                    for n, (w, x) in enumerate(PRODUCTS):
                        mm = nc.tensor.matmul(dense_bank(unit)[:, KVW * t:KVW * (t + 1)], X[x][:, c, P * t:P * (t + 1)],
                                              W[w][:, c, D + KVW:D + 2 * KVW], start=(c == 0 and n == 0),
                                              stop=(c == KC - 1 and n == 2))
                if t == TT - 1:
                    mm.then_inc(dense_ready, 1)

            def dense(b, kind, k, unit, piece):
                if kind == "T":
                    transposed_x(b, k, unit, piece)
                elif kind == "R":
                    project(k, unit, piece)
                else:
                    project_v(unit, piece)

            def scores(b, g, i, j):
                n = NKV * b + g
                r, q = g % RING, TT - 1 - i
                heads, width = HEADS_OF[i], CHUNK_N[i]
                u, place = j // heads, j % heads
                if i == 0 and j == 0:
                    pe.wait_ge(rows_staged[r], ROW_DMAS * (NKV // RING * b + g // RING + 1))
                before = BANKS_OF * n + BANK_AT[i] + u - S_BANKS + 1
                if place == 0 and positive(before):
                    pe.wait_ge(max_done, before)
                out = ps_s[:, (BANK_AT[i] + u) % S_BANKS, width * place:width * (place + 1)]
                nc.tensor.matmul(out, q_rows[r][0:PAIR, j, P * q:P * (q + 1)].bitcast(F32R),
                                 k_rows[r][0:PAIR, 0:width].bitcast(F32R), start=(place == 0), stop=False)
                if place == heads - 1:
                    diagonal = ps_s[:, (BANK_AT[i] + u) % S_BANKS, 0:heads * width].rearrange("p (j t) -> p j t", j=heads)[:, :, P * q:width]
                    nc.tensor.matmul(diagonal, ident_b[:], mask_q[:, 0:heads, :], start=False, stop=True
                                     ).then_inc(scores_ready, 1)

            def transposed_max(n, g, unit):
                pe.wait_ge(m_split, n + 1)
                bank_free(unit, 0)
                for q in range(TT):
                    mm = nc.tensor.transpose(ps_d[0:2 * GROUP, P * q:P * (q + 1)],
                                             m_parts[:, g % 2, q].rearrange("p w j -> p (w j)"), ident[:])
                mm.then_inc(dense_ready, 1)

            def scores_t(b, g, c, j):
                n = NKV * b + g
                r = g % RING
                heads, width = HEADS_OF[c], CHUNK_N[c]
                u, place = j // heads, j % heads
                if c == 0 and j == 0:
                    pe.wait_ge(m_staged[g % 2], DMA * (NKV // 2 * b + g // 2 + 1))
                before = BANKS_OF * n + BANK_AT[c] + u - S_BANKS + 1
                if place == 0 and positive(before):
                    pe.wait_ge(exp_done, before)
                bank = ps_t[:, (BANK_AT[c] + u) % S_BANKS, 0:heads * width].rearrange("p (j t) -> p j t", j=heads)
                nc.tensor.matmul(bank[:, place, :], k_rows[r][:, P * c:P * (c + 1)].bitcast(F32R),
                                 q_rows[r][:, j, P * c:T].bitcast(F32R), start=(place == 0), stop=False)
                if place == heads - 1:
                    nc.tensor.matmul(bank[:, :, 0:P], ident_b[:], mask_k[:, 0:heads, :], start=False,
                                     stop=True).then_inc(scores_t_ready, 1)

            def weighted_v(b, g, c):
                n = NKV * b + g
                pe.wait_ge(exp_done, BANKS_OF * n + BANK_AT[c + 1])
                if c == 0:
                    if positive(n):
                        pe.wait_ge(o_evacuated, n)
                    if g == 0:
                        pe.wait_ge(v_ready, b + 1)
                for j in range(GROUP):
                    mm = nc.tensor.matmul(ps_o[32 * j:32 * j + 2 * DH, P * c:T], v_ones[:, c, g, :],
                                          probs[:, g % 2, j, CHUNK_AT[c]:CHUNK_AT[c + 1]],
                                          start=(c == 0), stop=(c == TT - 1))
                if c == TT - 1:
                    mm.then_inc(pv_done, 1)

            def iteration(b, has_next):
                unit0 = UNITS * b + PRE_UNITS
                for slot in range(TT * NKV):
                    g, i = slot // TT, slot % TT
                    kind, k = UNIT_SLOT.get(slot, "--") if has_next else "--"
                    for j in range(GROUP):
                        if has_next or g < NKV - 2:
                            scores(b, g + 2, i, j)
                        scores_t(b, g, i, j)
                        if j == PV_AFTER[i] and i >= 1:
                            weighted_v(b, g, i - 1)
                        elif j == PV_AFTER[i] and g >= 1:
                            weighted_v(b, g - 1, TT - 1)
                        if i == 0 and j == MAX_AFTER and (has_next or g < NKV - 1):
                            transposed_max(NKV * b + g + 1, g + 1, unit0 + (UNIT_NO[slot] if has_next else g))
                        if kind == "T" and j == T_AFTER:
                            for t in range(TT):
                                transposed_x(b + 1, k, unit0 + UNIT_NO[slot], t)
                        elif kind in ("R", "V"):
                            for piece in range(4):
                                if PIECE_AFTER[i][piece] == j:
                                    dense(b + 1, kind, k, unit0 + UNIT_NO[slot], piece)
                weighted_v(b, NKV - 1, TT - 1)

            pe.wait_ge(consts_ready, 1)
            for unit in range(KC + N_ROPE + 1):
                kind = "T" if unit < KC else "R" if unit < KC + N_ROPE else "V"
                if unit == KC:
                    pe.wait_ge(w_split, KC)
                for piece in range(4):
                    dense(0, kind, unit - KC if kind == "R" else unit, unit, piece)
            for g in range(2):
                for i in range(TT):
                    for j in range(GROUP):
                        scores(0, g, i, j)
                    if g == 1 and i == 1:
                        transposed_max(0, 0, PRE_UNITS - 1)
            iteration(0, True)
            with pe.Fori(1, B - 1) as b:
                iteration(b, True)
            iteration(B - 1, False)


WO_SLOT = 3


def ring_units(has_next):
    units = []
    for f in range(FT):
        units += [("gate", f), ("up", f)]
        if has_next and 0 <= f - WO_SLOT < TT:
            units.append(("wo", f - WO_SLOT))
    if has_next:
        units += [("T", kc) for kc in range(KC)]
    return {u: n for n, u in enumerate(units)}


BANKS = 4
RING_PRE = {u: n for n, u in enumerate([("wo", t) for t in range(TT)] + [("T", c) for c in range(KC)])}
RING_FULL = ring_units(True)
RING_LAST = ring_units(False)
assert len(RING_PRE) % BANKS == 0


def phase_2(nc, d, to):
    with ExitStack() as ctx:
        def sb(name, shape, dt=F32):
            return ctx.enter_context(nc.sbuf_tensor(name, shape, dt))

        def sem(name):
            return ctx.enter_context(nc.semaphore(name))

        wg = [sb(f"wg_{p}", [P, KC, F], F32R) for p in ("hi", "lo")]
        wu = [sb(f"wu_{p}", [P, KC, F], F32R) for p in ("hi", "lo")]
        wd = [sb(f"wd_{p}", [P, FT, D], F32R) for p in ("hi", "lo")]
        ident = to.ident
        half = sb("half2", [P, 1])
        eps = sb("eps2", [P, 1])
        wo, o_in, inverse, x_res = to.wo, to.o_in, to.inverse, to.x_res
        xn = sb("xn2", [P, TT, D])
        y = sb("y", [P, TT, D])
        stats = sb("stats2", [P, 6])
        mean_var = sb("mean_var2", [P, 2])
        var_eps = sb("var_eps2", [P, 1])
        rstd = sb("rstd2", [P, 1])
        xt = [sb(f"x2t_{p}", [P, KC, T], F32R) for p in ("hi", "lo")]
        h = sb("h", [P, 2, T])
        sums = h[:, 1, 0:P]
        h_parts = [sb(f"h_{p}", [P, 2, T], F32R) for p in ("hi", "lo")]
        bank = [ctx.enter_context(nc.psum_tensor(f"bank{k}", [P, T], F32)) for k in range(BANKS)]
        ps_y = ctx.enter_context(nc.psum_tensor("ps_y", [P, TT, D], F32))

        consts_ready = sem("consts2_ready")
        ffn_loaded = [sem(f"ffn_loaded{f}") for f in range(FT)]
        ffn_hi_ready = sem("ffn_hi_ready")
        ffn_split = sem("ffn_split")
        sums_loaded = sem("sums2_loaded")
        inverse_stored = sem("inverse2_stored")
        recip_done = sem("recip_done")
        wo_done = sem("wo_done")
        x1_ready = sem("x1_ready")
        x1_stored = sem("x1_stored")
        ln_stats = sem("ln2_stats")
        ln_mean = sem("ln2_mean")
        var_ready = sem("var2_ready")
        rstd_ready = sem("rstd2_ready")
        xn_ready = sem("xn2_ready")
        xt_done = sem("x2t_done")
        xt_hi_ready = sem("x2t_hi_ready")
        xt_ready = sem("x2t_ready")
        gate_ready = sem("gate_ready")
        up_ready = sem("up_ready")
        silu_done = sem("silu_done")
        h_ready = sem("h_ready")
        h_hi_ready = sem("h_hi_ready")
        h_lo_ready = sem("h_lo_ready")
        down_done = sem("down_done")
        y_loaded = sem("y_loaded")
        y_evacuated = sem("y_evacuated")
        y_stored = sem("y_stored")

        W_DMAS = 3 * DMA

        def ctx_parts(b, t):
            if isinstance(b, int) and b == 0 and t in (1, 2):
                return [p[:, t - 1].rearrange("p (c t) -> p c t", c=QT) for p in h_parts]
            return [p[:] for p in to.ctx]

        block = ctx.enter_context(nc.Block())

        @block.sync
        def _(sp):
            def load_next_o(b, t):
                sp.wait_ge(to.ctx_lo_ready, TT * b + t - 1)
                load_o(sp, d, to, b, t)

            def load_next_residual(b, t):
                sp.wait_ge(x1_ready, TT * b + t - 1)
                load_residual(sp, d, to, b, t)

            def load_ffn(f):
                m = FW[f]
                for w, name in ((wg, "wg_raw"), (wu, "wu_raw")):
                    sp.dma_start(w[1][:, :, P * f:P * f + m].bitcast(F32),
                                 d[name].rearrange("(c p) n -> p c n", p=P)[:, :, P * f:P * f + m]
                                 ).then_inc(ffn_loaded[f], DMA)
                sp.dma_start(wd[1][0:m, f].bitcast(F32), d["wd_raw"][P * f:P * f + m]).then_inc(ffn_loaded[f], DMA)

            def store_x1(b, t):
                sp.wait_ge(x1_ready, TT * b + t + 1)
                sp.dma_start(d["x1"][b, P * t:P * (t + 1)], xn[:, t]).then_inc(x1_stored, DMA)

            def iteration(b, has_next):
                if positive(b):
                    sp.wait_ge(y_stored, TT * DMA * b)
                    sp.wait_ge(x1_stored, TT * DMA * b)
                    sp.dma_start(y[:], d["x1"][b].rearrange("(t p) n -> p t n", p=P)).then_inc(y_loaded, DMA)
                if has_next:
                    for t in range(2):
                        load_next_o(b + 1, t)
                        load_next_residual(b + 1, t)
                    for t in range(TT):
                        if t + 2 < TT:
                            load_next_o(b + 1, t + 2)
                        store_x1(b + 1, t)
                        if t + 2 < TT:
                            load_next_residual(b + 1, t + 2)
                for t in range(TT):
                    sp.wait_ge(y_evacuated, TT * b + t + 1)
                    sp.dma_start(d["out"][b, P * t:P * (t + 1)], y[:, t]).then_inc(y_stored, DMA)

            load_ffn(0)
            sp.dma_start(sums, row_sums(d, B - 1)).then_inc(sums_loaded, DMA)
            load_next_o(0, 3)
            load_ffn(1)
            for t in range(2, TT):
                load_next_residual(0, t)
            sp.wait_ge(recip_done, 1)
            sp.dma_start(row_inverses(d, B - 1), sums).then_inc(inverse_stored, DMA)
            for f in range(2, FT):
                load_ffn(f)
            iteration(0, True)
            with sp.Fori(1, B - 1) as b:
                iteration(b, True)
            iteration(B - 1, False)
            sp.wait_ge(y_stored, TT * DMA * B)
            sp.wait_ge(inverse_stored, DMA)
            sp.wait_ge(x1_stored, TT * DMA * (B - 1))

        @block.gpsimd
        def _(pool):
            pool.memset(half[:], -0.5)
            pool.memset(eps[:], EPS).then_inc(consts_ready, 1)
            pool.wait_ge(consts_ready, 1)
            with pool.Fori(0, B * TT) as n:
                pool.wait_ge(ln_mean, n + 1)
                nc.gpsimd.tensor_tensor(var_eps[:], mean_var[:, 1:2], eps[:], ALU.add).then_inc(var_ready, 1)
                pool.wait_ge(var_ready, n + 1)
                nc.gpsimd.tensor_tensor(rstd[:], var_eps[:], half[:], ALU.pow).then_inc(rstd_ready, 1)

        @block.scalar
        def _(act):
            def split_ffn_hi(f):
                act.wait_ge(ffn_loaded[f], W_DMAS)
                m = FW[f]
                for w in (wg, wu):
                    nc.scalar.copy(w[0][:, :, P * f:P * f + m], w[1][:, :, P * f:P * f + m].bitcast(F32)
                                   ).then_inc(ffn_hi_ready, 1)
                nc.scalar.copy(wd[0][0:m, f], wd[1][0:m, f].bitcast(F32)).then_inc(ffn_hi_ready, 1)

            def ctx_hi(b, t):
                n = TT * b + t
                if not isinstance(b, int) or b > 0 or t == 3:
                    act.wait_ge(wo_done, 1 if isinstance(n, int) and n == 3 else n)
                ctx_high(act, to, b, t, ctx_parts(b, t))

            def xt_hi(b, kc, units):
                act.wait_ge(xt_done, KC * b + kc + 1)
                nc.scalar.copy(xt[0][:, kc], bank[units["T", kc] % BANKS][:]).then_inc(xt_hi_ready, 1)

            def iteration(b, has_next):
                units = RING_FULL if has_next else RING_LAST
                first = isinstance(b, int) and b == 0
                for f in range(FT):
                    n, m, r = FT * b + f, FW[f], f % 2
                    act.wait_ge(gate_ready, n + 1)
                    if first and f == 1:
                        act.wait_ge(inverse_stored, DMA)
                    if not first or f >= 2:
                        act.wait_ge(h_lo_ready, FT * b if f < 2 else n - 1)
                    nc.scalar.activation(h[0:m, r], bank[units["gate", f] % BANKS][0:m, :], ACT.Silu
                                         ).then_inc(silu_done, 1)
                    act.wait_ge(h_ready, n + 1)
                    if not first or f >= 2:
                        act.wait_ge(down_done, FT * b if f < 2 else n - 1)
                    nc.scalar.copy(h_parts[0][0:m, r], h[0:m, r]).then_inc(h_hi_ready, 1)
                    if first and f + 2 < FT:
                        split_ffn_hi(f + 2)
                    if has_next and 0 <= f - WO_SLOT + 1 < TT:
                        ctx_hi(b + 1, f - WO_SLOT + 1)
                if has_next:
                    for kc in range(KC):
                        xt_hi(b + 1, kc, units)

            ctx_hi(0, 1)
            ctx_hi(0, 2)
            split_ffn_hi(0)
            ctx_hi(0, 3)
            split_ffn_hi(1)
            for kc in range(KC):
                xt_hi(0, kc, RING_PRE)
            iteration(0, True)
            with act.Fori(1, B - 1) as b:
                iteration(b, True)
            iteration(B - 1, False)

        @block.vector
        def _(dve):
            def split_ffn_lo(f):
                m = FW[f]
                for k, w in enumerate((wg, wu)):
                    at = P * f
                    dve.wait_ge(ffn_hi_ready, 3 * f + k + 1)
                    nc.vector.tensor_tensor(w[1][:, :, at:at + m], w[1][:, :, at:at + m].bitcast(F32),
                                            w[0][:, :, at:at + m].bitcast(F32), ALU.subtract).then_inc(ffn_split, 1)
                dve.wait_ge(ffn_hi_ready, 3 * f + 3)
                nc.vector.tensor_tensor(wd[1][0:m, f], wd[1][0:m, f].bitcast(F32), wd[0][0:m, f].bitcast(F32),
                                        ALU.subtract).then_inc(ffn_split, 1)

            def residual(b, t, units, x1):
                n = TT * b + t
                dve.wait_ge(wo_done, n + 1)
                dve.wait_ge(to.xres_loaded[t % 2], DMA * (TT // 2 * b + t // 2 + 1))
                k = units["wo", t] % BANKS
                nc.vector.tensor_tensor(x1[:, t], bank[k][:], x_res[:, t % 2], ALU.add).then_inc(x1_ready, 1)

            def statistics(n, t, x1):
                dve.wait_ge(x1_ready, n + 1)
                nc.vector.bn_stats(stats[:], x1[:, t]).then_inc(ln_stats, 1)

            def mean():
                nc.vector.bn_aggr(mean_var[:], stats[:]).then_inc(ln_mean, 1)

            def normalise(b, t):
                n = TT * b + t
                x1 = xn if positive(b) else y
                dve.wait_ge(rstd_ready, n + 1)
                if positive(b):
                    dve.wait_ge(x1_stored, DMA * (n + 1 - TT))
                nc.vector.tensor_scalar(xn[:, t], x1[:, t], mean_var[:, 0:1], rstd[:, 0:1], ALU.subtract,
                                        ALU.mult).then_inc(xn_ready, 1)

            def xt_lo(b, kc, units):
                k = units["T", kc] % BANKS
                dve.wait_ge(xt_hi_ready, KC * b + kc + 1)
                nc.vector.tensor_tensor(xt[1][:, kc], bank[k][:], xt[0][:, kc].bitcast(F32),
                                        ALU.subtract).then_inc(xt_ready, 1)

            def iteration(b, has_next):
                units = RING_FULL if has_next else RING_LAST
                first = isinstance(b, int) and b == 0
                for f in range(FT):
                    n, m, r = FT * b + f, FW[f], f % 2
                    stats_of = f - WO_SLOT - 2
                    normalised = has_next and 0 <= stats_of < TT
                    if normalised:
                        dve.wait_ge(ln_stats, TT * (b + 1) + stats_of + 1)
                    dve.wait_ge(silu_done, n + 1)
                    dve.wait_ge(up_ready, n + 1)
                    nc.vector.tensor_tensor(h[0:m, r], h[0:m, r], bank[units["up", f] % BANKS][0:m, :],
                                            ALU.mult).then_inc(h_ready, 1)
                    if normalised:
                        mean()
                    dve.wait_ge(h_hi_ready, n + 1)
                    nc.vector.tensor_tensor(h_parts[1][0:m, r], h[0:m, r], h_parts[0][0:m, r].bitcast(F32),
                                            ALU.subtract).then_inc(h_lo_ready, 1)
                    if first and f + 2 < FT:
                        split_ffn_lo(f + 2)
                    if normalised:
                        normalise(b + 1, stats_of)
                    if has_next:
                        t = f - WO_SLOT + 1
                        if 0 <= t - 2 < TT:
                            residual(b + 1, t - 2, units, xn)
                            statistics(TT * (b + 1) + t - 2, t - 2, xn)
                        if 0 <= t < TT:
                            scale_ctx(dve, to, b + 1, t)
                            ctx_low(dve, to, b + 1, t, ctx_parts(b + 1, t))
                if has_next:
                    for kc in range(KC):
                        xt_lo(b + 1, kc, units)
                if positive(b):
                    dve.wait_ge(y_loaded, DMA * b)
                dve.wait_ge(down_done, FT * (b + 1))
                for t in range(TT):
                    nc.vector.tensor_tensor(y[:, t], ps_y[:, t], y[:, t], ALU.add).then_inc(y_evacuated, 1)

            ctx_low(dve, to, 0, 1, ctx_parts(0, 1))
            scale_ctx(dve, to, 0, 2)
            ctx_low(dve, to, 0, 2, ctx_parts(0, 2))
            split_ffn_lo(0)
            for t in range(TT):
                residual(0, t, RING_PRE, y)
                if t >= 1:
                    normalise(0, t - 1)
                statistics(t, t, y)
                if t == 0:
                    scale_ctx(dve, to, 0, 3)
                    ctx_low(dve, to, 0, 3, ctx_parts(0, 3))
                dve.wait_ge(ln_stats, t + 1)
                mean()
            normalise(0, TT - 1)
            dve.wait_ge(sums_loaded, DMA)
            nc.vector.reciprocal(sums, sums).then_inc(recip_done, 1)
            split_ffn_lo(1)
            for kc in range(KC):
                xt_lo(0, kc, RING_PRE)
            iteration(0, True)
            with dve.Fori(1, B - 1) as b:
                iteration(b, True)
            iteration(B - 1, False)

        @block.tensor
        def _(pe):
            PRODUCTS = ((0, 0), (0, 1), (1, 0))

            def three_products(out, weights, moving, chunks):
                for c in range(chunks):
                    for n, (w, m) in enumerate(PRODUCTS):
                        mm = nc.tensor.matmul(out, weights(w, c), moving(m, c), start=(c == 0 and n == 0),
                                              stop=(c == chunks - 1 and n == 2))
                return mm

            def wait_bank(unit, units, b):
                order = list(units)
                if unit >= BANKS:
                    name, t = order[unit - BANKS]
                    wait_read(name, t, b, units)
                elif units is not RING_PRE:
                    k = unit % BANKS
                    if isinstance(b, int) and b == 0:
                        name, t = list(RING_PRE)[len(RING_PRE) - BANKS + k]
                    else:
                        name, t = [u for u, q in RING_FULL.items() if q % BANKS == k][-1]
                    wait_read(name, t, b - 1, None)

            def wait_read(name, t, b, units):
                ahead = 0 if units is RING_PRE else 1
                if name == "gate":
                    pe.wait_ge(silu_done, FT * b + t + 1)
                elif name == "up":
                    pe.wait_ge(h_ready, FT * b + t + 1)
                elif name == "wo":
                    pe.wait_ge(x1_ready, TT * (b + ahead) + t + 1)
                else:
                    pe.wait_ge(xt_ready, KC * (b + ahead) + t + 1)

            def project_out(b, t, units, at):
                unit = units["wo", t]
                pe.wait_ge(to.ctx_lo_ready, TT * b + t + 1)
                wait_bank(unit, units, at)
                three_products(bank[unit % BANKS][:], lambda w, c: ctx_parts(b, t)[w][:, c, :], lambda m, c: wo[m][:, c, :],
                               KC).then_inc(wo_done, 1)

            def transposed_x(b, kc, units, at):
                unit = units["T", kc]
                pe.wait_ge(xn_ready, TT * (b + 1))
                wait_bank(unit, units, at)
                for t in range(TT):
                    mm = nc.tensor.transpose(bank[unit % BANKS][:, P * t:P * (t + 1)],
                                             xn[:, t, P * kc:P * (kc + 1)], ident[:])
                mm.then_inc(xt_done, 1)

            def down(b, f):
                n, m, r = FT * b + f, FW[f], f % 2
                pe.wait_ge(h_lo_ready, n + 1)
                if f == 0 and (not isinstance(b, int) or b > 0):
                    pe.wait_ge(y_evacuated, TT * b)
                for t in range(TT):
                    for k, (w, p) in enumerate(PRODUCTS):
                        mm = nc.tensor.matmul(ps_y[:, t], h_parts[w][0:m, r, P * t:P * (t + 1)], wd[p][0:m, f, :],
                                              start=(f == 0 and k == 0), stop=(f == FT - 1 and k == 2))
                mm.then_inc(down_done, 1)

            def iteration(b, has_next):
                units = RING_FULL if has_next else RING_LAST
                first = isinstance(b, int) and b == 0
                pe.wait_ge(xt_ready, KC * (b + 1))
                for f in range(FT):
                    m = FW[f]
                    if first:
                        pe.wait_ge(ffn_split, 3 * (f + 1))
                    for name, w, ready in (("gate", wg, gate_ready), ("up", wu, up_ready)):
                        unit = units[name, f]
                        wait_bank(unit, units, b)
                        three_products(bank[unit % BANKS][0:m, :], lambda q, c: w[q][:, c, P * f:P * f + m],
                                       lambda q, c: xt[q][:, c, :], KC).then_inc(ready, 1)
                    if has_next and 0 <= f - WO_SLOT < TT:
                        project_out(b + 1, f - WO_SLOT, units, b)
                    if f >= 1:
                        down(b, f - 1)
                if has_next:
                    for kc in range(KC):
                        transposed_x(b + 1, kc, units, b)
                down(b, FT - 1)

            pe.wait_ge(to.wo_split, KC)
            for t in range(TT):
                project_out(0, t, RING_PRE, 0)
            for kc in range(KC):
                transposed_x(0, kc, RING_PRE, 0)
            iteration(0, True)
            with pe.Fori(1, B - 1) as b:
                iteration(b, True)
            iteration(B - 1, False)


def build(nc, d):
    with ExitStack() as ctx:
        handover = Handover(nc, ctx)
        phase_1(nc, d, handover)
        phase_2(nc, d, handover)


def rope_tables():
    import numpy as np
    f = np.float32
    theta, factor, lo, hi, length = 500000.0, 32.0, 1.0, 4.0, 1024
    at = np.arange(0, DH, 2, dtype=f) / f(DH)
    freq = f(1.0 / (2.0 * np.pi)) * np.power(f(theta), -at)
    low, high = f(lo / length), f(hi / length)
    scaled = np.where(freq < low, freq / f(factor), freq)
    smooth = np.clip((f(length) * freq - f(lo)) / f(hi - lo), f(0), f(1))
    blended = (f(1) - smooth) * (freq / f(factor)) + smooth * freq
    freq = np.where((freq >= low) & (freq <= high), blended, scaled).astype(f)
    phase = f(2.0 * np.pi) * np.arange(T, dtype=f)[None, :] * freq[:, None]
    cos, sin = np.cos(phase), np.sin(phase)
    heads = P // DH
    return (np.tile(np.concatenate([cos, cos]), (heads, 1)).astype(f),
            np.tile(np.concatenate([-sin, sin]), (heads, 1)).astype(f))


def kernel(L0_attn_resid, L0_attn_Wq, L0_attn_Wk, L0_attn_Wv, L0_attn_Wo, L0_ffn_W_gate, L0_ffn_W_up,
           L0_ffn_W_down):
    import numpy as np
    import concourse.bacc as bacc
    from concourse.bass_utils import run_bass_kernel_spmd

    nc = bacc.Bacc("TRN2", target_bir_lowering=False, num_devices=1)
    cos, sin = rope_tables()
    given = {"x": L0_attn_resid, "wq": L0_attn_Wq, "wk": L0_attn_Wk, "wv": L0_attn_Wv, "wo": L0_attn_Wo,
             "wg": np.asarray(L0_ffn_W_gate).T, "wu": np.asarray(L0_ffn_W_up).T,
             "wd": np.asarray(L0_ffn_W_down).T, "cos": cos, "sin": sin}
    arrays, d = {}, {}
    for name, a in given.items():
        a = np.ascontiguousarray(a)
        arrays[f"in_{name}"] = a
        d[name] = nc.dram_tensor(f"in_{name}", a.shape, F32, kind="ExternalInput").ap()
    for name, shape in (("q_parts", (B, D // DH, 3, DH, T)), ("k_parts", (B, NKV, 3, DH, T)),
                        ("o", (B, NKV, P, T)), ("inverse", (B, NKV * GROUP, T)), ("x1", (B, T, D)), ("wo_raw", (D, D)), ("wg_raw", (D, F)),
                        ("wu_raw", (D, F)), ("wd_raw", (F, D))):
        d[name] = nc.dram_tensor(f"scratch_{name}", shape, F32, kind="Internal").ap()
    d["out"] = nc.dram_tensor("out", (B, T, D), F32, kind="ExternalOutput").ap()
    build(nc, d)
    r = run_bass_kernel_spmd(nc, [arrays], core_ids=[0])
    return r.results[0]["out"]
```
